# Optimizing a Trainium2 kernel written in Bass

```python
import numpy as np
import jax
import jax.numpy as jnp

def _softmax(x, axis=-1):
    return jax.nn.softmax(x, axis=axis)

def _gelu(x):
    return jax.nn.gelu(x, approximate=True)

def _silu(x):
    return jax.nn.silu(x)

def _sigmoid(x):
    return jax.nn.sigmoid(x)

def _layernorm(x, axis=-1, eps=1e-05):
    m = jnp.mean(x, axis=axis, keepdims=True)
    v = jnp.var(x, axis=axis, keepdims=True)
    return (x - m) / jnp.sqrt(v + eps)

def _scatter_add(tgt, idx, src, axis=0):
    return tgt.at[idx].add(src)

def _segment_sum(src, seg, n):
    return jax.ops.segment_sum(src, seg, n)
kernel_name = 'mk_recurrent_d1_jaxref_r4_60fa6e'

def setup_inputs(seed: int=0):
    np.random.seed(seed)
    _w = jnp.asarray

    def _L0_attn_setup():
        import jax, jax.numpy as jnp
        import numpy as np
        import math
        B, S, D = (4, 1024, 512)
        H, HEAD_DIM = (16, 96)
        D3 = HEAD_DIM // 3

        def _flash_attention(q, k, v, use_causal_mask=True):
            seq_len = q.shape[-2]
            block_size = min(64, seq_len)
            d = q.shape[-1]
            out = jnp.zeros_like(q)
            for i in range(0, seq_len, block_size):
                qb = q[..., i:i + block_size, :]
                kb = k[..., :i + block_size, :]
                vb = v[..., :i + block_size, :]
                scores = jnp.einsum('...hqd,...hkd->...hqk', qb, kb, precision=jax.lax.Precision.HIGHEST)
                scores = scores / jnp.sqrt(jnp.float32(d))
                if use_causal_mask:
                    mask = jnp.tril(jnp.ones((qb.shape[-2], kb.shape[-2]), dtype=jnp.float32))
                    scores = jnp.where(mask == 0, -1000000000.0, scores)
                w = jax.nn.softmax(scores, axis=-1)
                ob = jnp.einsum('...hqk,...hvd->...hqd', w, vb, precision=jax.lax.Precision.HIGHEST)
                out = out.at[..., i:i + block_size, :].set(ob)
            return out
        key = jax.random.key(seed)
        k0, k1, k2 = jax.random.split(key, 3)
        x = jax.random.normal(k0, (B, S, D), dtype=jnp.float32)
        Wqkv = jax.random.normal(k1, (D, H, HEAD_DIM), dtype=jnp.float32) / math.sqrt(D)
        bqkv = jnp.zeros((H, HEAD_DIM), dtype=jnp.float32)
        Wout = jax.random.normal(k2, (H, D3, D), dtype=jnp.float32) / math.sqrt(H * D3)
        bout = jnp.zeros((D,), dtype=jnp.float32)
        return {'x': x, 'Wqkv': Wqkv, 'bqkv': bqkv, 'Wout': Wout, 'bout': bout}
    _L0_attn_in = _L0_attn_setup()

    def _L0_ffn_setup():
        import jax, jax.numpy as jnp
        import numpy as np
        B, S, D = (4, 512, 512)
        E, K, M = (8, 2, 256)
        key = jax.random.key(seed)
        k0, k1, k2, k3, k4 = jax.random.split(key, 5)
        d_scale = D ** (-0.5)
        m_scale = M ** (-0.5)
        return {'x': jax.random.normal(k0, (B, S, D), jnp.float32), 'w_gate': jax.random.normal(k1, (D, E), jnp.float32) * d_scale, 'wi_0': jax.random.normal(k2, (E, D, M), jnp.float32) * d_scale, 'wi_1': jax.random.normal(k3, (E, D, M), jnp.float32) * d_scale, 'wo': jax.random.normal(k4, (E, M, D), jnp.float32) * m_scale}
    _L0_ffn_in = _L0_ffn_setup()
    _d = {'L0_attn_x': _L0_attn_in['x'], 'L0_attn_Wqkv': _L0_attn_in['Wqkv'], 'L0_attn_bqkv': _L0_attn_in['bqkv'], 'L0_attn_Wout': _L0_attn_in['Wout'], 'L0_attn_bout': _L0_attn_in['bout'], 'L0_ffn_w_gate': _L0_ffn_in['w_gate'], 'L0_ffn_wi_0': _L0_ffn_in['wi_0'], 'L0_ffn_wi_1': _L0_ffn_in['wi_1'], 'L0_ffn_wo': _L0_ffn_in['wo']}
    _x0 = _d['L0_attn_x']
    _d['L0_attn_x'] = jax.random.normal(jax.random.fold_in(jax.random.key(seed), 1), (2, 4096, 512), dtype=_x0.dtype)
    del _x0
    return _d

def reference(L0_attn_x, L0_attn_Wqkv, L0_attn_bqkv, L0_attn_Wout, L0_attn_bout, L0_ffn_w_gate, L0_ffn_wi_0, L0_ffn_wi_1, L0_ffn_wo):

    def _L0_attn_ref(x, Wqkv, bqkv, Wout, bout):
        import jax, jax.numpy as jnp
        import numpy as np
        import math
        B, S, D = (4, 1024, 512)
        H, HEAD_DIM = (16, 96)
        D3 = HEAD_DIM // 3

        def _flash_attention(q, k, v, use_causal_mask=True):
            seq_len = q.shape[-2]
            block_size = min(64, seq_len)
            d = q.shape[-1]
            out = jnp.zeros_like(q)
            for i in range(0, seq_len, block_size):
                qb = q[..., i:i + block_size, :]
                kb = k[..., :i + block_size, :]
                vb = v[..., :i + block_size, :]
                scores = jnp.einsum('...hqd,...hkd->...hqk', qb, kb, precision=jax.lax.Precision.HIGHEST)
                scores = scores / jnp.sqrt(jnp.float32(d))
                if use_causal_mask:
                    mask = jnp.tril(jnp.ones((qb.shape[-2], kb.shape[-2]), dtype=jnp.float32))
                    scores = jnp.where(mask == 0, -1000000000.0, scores)
                w = jax.nn.softmax(scores, axis=-1)
                ob = jnp.einsum('...hqk,...hvd->...hqd', w, vb, precision=jax.lax.Precision.HIGHEST)
                out = out.at[..., i:i + block_size, :].set(ob)
            return out
        qkv = jnp.einsum('bsm,mhd->bshd', x, Wqkv, precision=jax.lax.Precision.HIGHEST) + bqkv
        q, k, v = jnp.split(qkv, 3, axis=-1)
        attn = _flash_attention(q, k, v, use_causal_mask=True)
        y = jnp.einsum('bshd,hdm->bsm', attn, Wout, precision=jax.lax.Precision.HIGHEST) + bout
        return y

    def _L0_ffn_ref(x, w_gate, wi_0, wi_1, wo):
        import jax, jax.numpy as jnp
        import numpy as np
        B, S, D = (4, 512, 512)
        E, K, M = (8, 2, 256)
        b, s, d = x.shape
        e = w_gate.shape[1]
        xf = x.reshape(-1, d)
        logits = jnp.dot(xf, w_gate)
        top_logits, top_idx = jax.lax.top_k(logits, K)
        weights = jax.nn.softmax(top_logits, axis=-1)
        flat_idx = top_idx.reshape(-1)
        sort_order = jnp.argsort(flat_idx)
        token_ids = sort_order // K
        sorted_x = jnp.take(xf, token_ids, axis=0)
        group_sizes = jnp.bincount(flat_idx, length=E).astype(jnp.int32)
        h0 = jax.lax.ragged_dot(sorted_x, wi_0, group_sizes)
        h1 = jax.lax.ragged_dot(sorted_x, wi_1, group_sizes)
        inter = jax.nn.silu(h0) * h1
        out_sorted = jax.lax.ragged_dot(inter, wo, group_sizes)
        unsort = jnp.argsort(sort_order)
        out = jnp.take(out_sorted, unsort, axis=0).reshape(-1, K, d)
        out = jnp.einsum('tkd,tk->td', out, weights)
        return out.reshape(b, s, d)
    x = L0_attn_x
    xn = _layernorm(x, axis=-1)
    s = _L0_attn_ref(xn, L0_attn_Wqkv, L0_attn_bqkv, L0_attn_Wout, L0_attn_bout)
    g = _silu(_L0_ffn_ref(xn, L0_ffn_w_gate, L0_ffn_wi_0, L0_ffn_wi_1, L0_ffn_wo))
    x = x + s * g
    return x

_drawn_inputs = setup_inputs


def setup_inputs(seed=0):
    import zlib

    import numpy as np

    out = dict(_drawn_inputs(seed))
    spreads = {'L0_attn_bqkv': (0.0, 0.1), 'L0_attn_bout': (0.0, 0.458)}
    factors = {}
    for name, (base, spread) in spreads.items():
        noise = np.random.default_rng([zlib.crc32(name.encode()), seed]).standard_normal(out[name].shape)
        drawn = base * np.exp(spread * noise) if base else spread * noise
        out[name] = jnp.asarray(drawn.astype(out[name].dtype))
    for name, factor in factors.items():
        out[name] = (out[name] * factor).astype(out[name].dtype)
    return out
```

```python
from contextlib import ExitStack

import concourse.bass as bass
import concourse.mybir as mybir
import numpy as np
from concourse.bass import IndirectOffsetOnAxis

F32, F32R, F16, BF16, I32 = (mybir.dt.float32, mybir.dt.float32r, mybir.dt.float16, mybir.dt.bfloat16,
                             mybir.dt.int32)
ALU = mybir.AluOpType
ACT = mybir.ActivationFunctionType
AX = mybir.AxisListType.X
REDUCE_MAX = bass.bass_isa.ReduceOp.max

P = 128
BATCH, SEQ, D = 2, 4096, 512
TOKENS = BATCH * SEQ
HEADS, DH = 16, 32
EXPERTS, TOPK, FF = 8, 2, 256
KD = D // P
KF = FF // P
HC = HEADS * DH // P
TILES = TOKENS // P
SLOT_TILES = TOKENS * TOPK // P + EXPERTS
REGION = TOKENS
EPS = 1e-5
GROUP = 32
GROUPS = P // GROUP
BLOCKS = P // (GROUPS * 2)
ROUTE_TILES = 8
XBUFS = 2
SIDE = DH + EXPERTS
MASKED = -1e9 * float(np.sqrt(DH))
SCORE_SCALE = 1.0 / float(np.sqrt(DH))
EXPONENT = 0x7F800000


def after(eng, sem, n):
    if not isinstance(n, int) or n > 0:
        eng.wait_ge(sem, n)


def in_range(i, n):
    return not isinstance(i, int) or 0 <= i < n


def turns(eng, body, first, last, end):
    for u in range(first):
        body(u)
    with eng.Fori(first, last) as u:
        body(u)
    for u in range(last, end):
        body(u)


class Steps:

    def __init__(self, eng, sem):
        self.eng, self.sem, self.base, self.n = eng, sem, 0, 0

    def did(self, ins):
        ins.then_inc(self.sem, 1)
        self.n += 1

    def wait(self):
        self.eng.wait_ge(self.sem, self.base + self.n)

    def turns(self, body, first, last, end, per_turn):
        for u in range(first):
            body(u)
        before, self.n = self.base + self.n, 0
        with self.eng.Fori(first, last) as u:
            self.base = (u - first) * per_turn + before
            body(u)
            assert self.n == per_turn, f"a turn of the loop has {self.n} signals"
        self.base, self.n = before + (last - first) * per_turn, 0
        for u in range(last, end):
            body(u)


def spread(ap, n):
    return ap.unsqueeze(2).to_broadcast([ap.shape[0], ap.shape[1], n])


def r32(ap):
    return ap.bitcast(F32)


def add_bias(bank, sb, tensor, n):
    rows = slice(GROUP * n, GROUP * n + 2)
    tensor.matmul(bank[:], sb["ones_r"][rows], sb["biases"][rows], start=True, stop=False)


def prepare(nc, dram, sb, banks):
    with ExitStack() as own:
        def t(name, shape, dt):
            return own.enter_context(nc.sbuf_tensor(name, shape, dt))

        def sem(name):
            return own.enter_context(nc.semaphore(name))

        raw = t("raw", [P, 2, 4, 512], F32)
        side = t("side", [P, KD, SIDE], F32)
        rowno, rowf = t("rowno", [P, 2], I32), t("rowf", [P, 3], F32)
        second = t("second", [P, BLOCKS, 2], F32)
        zeros = t("zeros", [P, EXPERTS * REGION // P], I32)
        mx, mxa = t("mx", [P, EXPERTS], F32), t("mxa", [P, EXPERTS], F32)
        rec = t("rec", [P, EXPERTS], F32)
        onesf = t("onesf", [P, P], F32)

        wg_in = sem("wg_in")
        raw_in = [sem("raw_in0"), sem("raw_in1")]
        raw_read = sem("raw_read")
        high_done = sem("high_done")
        consts = sem("consts")
        mx_ready, mxa_ready, scale_ready = sem("mx_ready"), sem("mxa_ready"), sem("scale_ready")
        dve_step, rows_ready = sem("prep_dve_step"), sem("rows_ready")
        stored = sem("prep_stored")

        ZEROED = 7
        items = [("bias", 0), ("proj", 0), ("proj", 1), ("wv", 0)] + [("max", e) for e in range(EXPERTS)]
        items += [("wi", e) for e in range(EXPERTS)] + [("wo", e) for e in range(0, EXPERTS, 2)]
        splits = [n for n, (kind, _) in enumerate(items) if kind not in ("bias", "max", "wv")]

        with nc.Block() as block:
            @block.sync
            def _(sp):
                sp.dma_start(side[:, :, DH:], dram["w_gate"].rearrange("(k p) e -> p k e", p=P)).then_inc(wg_in, 16)
                for n, (kind, e) in enumerate(items):
                    if n >= 2:
                        sp.wait_ge(raw_read, n - 1)
                    to = raw[:, n % 2]
                    if kind == "bias":
                        for i in range(0, 4, 2):
                            sp.dma_start(to[:, i:i + 2], dram["biases"][None, i:i + 2, :].to_broadcast([P, 2, D])
                                         ).then_inc(raw_in[n % 2], 16)
                    elif kind in ("proj", "wv"):
                        name = "wv" if kind == "wv" else ("wq", "wk")[e]
                        for i in range(2):
                            half = slice(KD // 2 * i, KD // 2 * (i + 1))
                            sp.dma_start(to[:, half], dram[name].rearrange("(k p) n -> p k n", p=P)[:, half]
                                         ).then_inc(raw_in[n % 2], 16)
                    elif kind == "wo":
                        for i in range(2):
                            sp.dma_start(to[:, KF * i:KF * i + KF, :],
                                         dram["wo"][e + i].rearrange("(k p) n -> p k n", p=P)
                                         ).then_inc(raw_in[n % 2], 16)
                    else:
                        for i in range(2):
                            sp.dma_start(to[:, :, FF * i:FF * i + FF],
                                         dram[f"wi_{i}"][e].rearrange("(k p) n -> p k n", p=P)
                                         ).then_inc(raw_in[n % 2], 16)
                sp.wait_ge(consts, ZEROED)
                sp.dma_start(dram["lists"].rearrange("(p n) o -> p (n o)", p=P), zeros[:]).then_inc(stored, 16)
                sp.wait_ge(stored, 16)

            @block.gpsimd
            def _(pool):
                g = nc.gpsimd
                g.memset(sb["ident"][:], 0.0).then_inc(consts, 1)
                g.memset(sb["ident_bf"][:], 0.0).then_inc(consts, 1)
                g.memset(sb["below"][:], 1.0).then_inc(consts, 1)
                g.memset(sb["ones_bf"][:], 1.0).then_inc(consts, 1)
                g.memset(sb["mask"][:], 0.0).then_inc(consts, 1)
                g.memset(onesf[:], 1.0).then_inc(consts, 1)
                g.memset(zeros[:], 0).then_inc(consts, 1)
                pool.wait_ge(consts, ZEROED)
                for m in (sb["ident"], sb["ident_bf"]):
                    g.affine_select(out=m[:], in_=m[:], compare_op=ALU.not_equal, fill=1.0, base=0,
                                    pattern=[[-1, P]], channel_multiplier=1).then_inc(consts, 1)
                g.affine_select(out=sb["below"][:], in_=sb["below"][:], compare_op=ALU.is_gt, fill=0.0,
                                base=0, pattern=[[1, P]], channel_multiplier=-1).then_inc(consts, 1)
                n = ZEROED + 3
                for b in range(GROUPS):
                    part = sb["mask"][GROUP * b:GROUP * b + GROUP]
                    pool.wait_ge(consts, n)
                    g.affine_select(out=part, in_=part, compare_op=ALU.is_ge, fill=MASKED, base=0,
                                    pattern=[[0, BLOCKS], [-1, 2 * HEADS]], channel_multiplier=1).then_inc(consts, 1)
                    pool.wait_ge(consts, n + 1)
                    first = part[:, :, 0:HEADS]
                    g.affine_select(out=first, in_=first, compare_op=ALU.is_ge, fill=MASKED, base=HEADS - 1,
                                    pattern=[[0, BLOCKS], [0, HEADS]], channel_multiplier=-1).then_inc(consts, 1)
                    n += 2
                pool.wait_ge(consts, n)
                g.iota(rowno[:], pattern=[[0, 2]], base=0, channel_multiplier=1).then_inc(rows_ready, 1)
                g.iota(second[:], pattern=[[0, BLOCKS], [HEADS, 2]], base=0, channel_multiplier=0,
                       allow_small_or_imprecise_dtypes=True).then_inc(rows_ready, 1)
                g.iota(sb["token"][:], pattern=[[P, TILES]], base=0, channel_multiplier=1)
                g.iota(sb["iota_e"][:], pattern=[[0, ROUTE_TILES], [1, EXPERTS]], base=-EXPERTS,
                       channel_multiplier=0, allow_small_or_imprecise_dtypes=True)
                g.iota(sb["count"][:], pattern=[[REGION, EXPERTS]], base=0, channel_multiplier=0,
                       allow_small_or_imprecise_dtypes=True)
                g.iota(sb["region"][:], pattern=[[REGION, EXPERTS]], base=0, channel_multiplier=0,
                       allow_small_or_imprecise_dtypes=True)
                pool.wait_ge(mx_ready, EXPERTS)
                g.partition_all_reduce(mxa[:], mx[:], P, REDUCE_MAX).then_inc(mxa_ready, 1)

            @block.scalar
            def _(act):
                a = nc.scalar
                for n, (kind, e) in enumerate(items):
                    if n not in splits:
                        continue
                    act.wait_ge(raw_in[n % 2], 32 * (n // 2 + 1))
                    if kind == "proj":
                        a.activation(sb[("proj", "wk")[e] + "_hi"][:], raw[:, n % 2], ACT.Copy).then_inc(high_done, 1)
                    elif kind == "wo":
                        a.activation(sb["wo_hi"][:, e:e + 2].rearrange("p e k n -> p (e k) n"),
                                     raw[:, n % 2], ACT.Copy).then_inc(high_done, 1)
                    else:
                        if e == 0:
                            act.wait_ge(scale_ready, 1)
                        a.activation(sb["wi_hi"][:, e], raw[:, n % 2], ACT.Identity,
                                     scale=sb["wi_scale"][:, e:e + 1]).then_inc(high_done, 1)

            @block.vector
            def _(dve):
                v = nc.vector
                st = Steps(dve, dve_step)
                dve.wait_ge(consts, ZEROED)
                st.did(v.tensor_copy(sb["ones_r"][:], onesf[:]))
                dve.wait_ge(rows_ready, 2)
                st.did(v.tensor_scalar(rowno[:, 0:1], rowno[:, 0:1], GROUP - 1, None, ALU.bitwise_and))
                st.did(v.tensor_scalar(rowno[:, 1:2], rowno[:, 1:2], HEADS, None, ALU.bitwise_and)); st.wait()
                st.did(v.tensor_scalar(rowf[:, 0:1], rowno[:, 0:1], 0.0, None, ALU.is_equal))
                st.did(v.tensor_scalar(rowf[:, 1:2], rowno[:, 0:1], 1.0, None, ALU.is_equal))
                st.did(v.tensor_copy(rowf[:, 2:3], rowno[:, 1:2])); st.wait()
                st.did(v.tensor_scalar(sb["same_token"][:], second[:], rowf[:, 2:3], None, ALU.is_equal))
                for n, (kind, e) in enumerate(items):
                    item = raw[:, n % 2]
                    dve.wait_ge(raw_in[n % 2], 32 * (n // 2 + 1))
                    if kind == "bias":
                        names = ("bq", "bk", "bout")
                        st.did(v.tensor_reduce(sb["bv"][:], item[:, 3].rearrange("p (h d) -> p d h", d=DH), AX, ALU.add))
                        for i, name in enumerate(names):
                            rows = slice(GROUP * i, GROUP * i + GROUP)
                            st.did(v.tensor_copy(sb["biases"][rows], item[rows, i])); st.wait()
                            st.did(v.tensor_tensor(item[rows, i], item[rows, i], r32(sb["biases"][rows]), ALU.subtract))
                            st.wait()
                        st.did(v.tensor_scalar(item[:, 0:3], item[:, 0:3], rowf[:, 1:2], None, ALU.mult)); st.wait()
                        for i, name in enumerate(names):
                            rows = slice(GROUP * i, GROUP * i + GROUP)
                            st.did(v.scalar_tensor_tensor(out=sb["biases"][rows], in0=r32(sb["biases"][rows]),
                                                          scalar=rowf[rows, 0:1], in1=item[rows, i],
                                                          op0=ALU.mult, op1=ALU.add))
                        st.wait()
                        dve.sem_inc(raw_read, 1)
                        continue
                    if kind == "wv":
                        for k in range(KD):
                            last = v.tensor_reduce(side[:, k, 0:DH], item[:, k].rearrange("p (h d) -> p d h", d=DH),
                                                   AX, ALU.add)
                        last.then_inc(raw_read, 1)
                        dve.wait_ge(raw_read, n + 1)
                        dve.wait_ge(wg_in, 16)
                        st.did(v.tensor_copy(sb["side_hi"][:], side[:])); st.wait()
                        st.did(v.tensor_tensor(sb["side_lo"][:], side[:], r32(sb["side_hi"][:]), ALU.subtract))
                        continue
                    if kind == "max":
                        v.tensor_reduce(mx[:, e:e + 1], item.rearrange("p k n -> p (k n)"), AX, ALU.max,
                                        apply_absolute_value=True).then_inc(mx_ready, 1)
                        dve.wait_ge(mx_ready, e + 1)
                        dve.sem_inc(raw_read, 1)
                        if e == EXPERTS - 1:
                            dve.wait_ge(mxa_ready, 1)
                            st.did(v.tensor_scalar(mxa[:], mxa[:], 1e-30, None, ALU.max)); st.wait()
                            st.did(v.tensor_scalar(mxa[:].bitcast(I32), mxa[:].bitcast(I32), EXPONENT, None,
                                                   ALU.bitwise_and)); st.wait()
                            st.did(v.reciprocal(rec[:], mxa[:]))
                            st.did(v.tensor_scalar(sb["wi_inv"][:], mxa[:], 2.0 ** -14, None, ALU.mult)); st.wait()
                            v.tensor_scalar(sb["wi_scale"][:], rec[:], 2.0 ** 14, None, ALU.mult).then_inc(scale_ready, 1)
                            dve.wait_ge(scale_ready, 1)
                        continue
                    dve.wait_ge(high_done, splits.index(n) + 1)
                    if kind == "proj":
                        ins = v.tensor_tensor(sb[("proj", "wk")[e] + "_lo"][:], item,
                                              r32(sb[("proj", "wk")[e] + "_hi"][:]), ALU.subtract)
                    elif kind == "wo":
                        ins = v.tensor_tensor(sb["wo_lo"][:, e:e + 2].rearrange("p e k n -> p (e k) n"), item,
                                              r32(sb["wo_hi"][:, e:e + 2]).rearrange("p e k n -> p (e k) n"),
                                              ALU.subtract)
                    else:
                        ins = v.scalar_tensor_tensor(out=sb["wi_lo"][:, e], in0=item,
                                                     scalar=sb["wi_scale"][:, e:e + 1], in1=sb["wi_hi"][:, e],
                                                     op0=ALU.mult, op1=ALU.subtract)
                    ins.then_inc(raw_read, 1)


def attend_and_route(nc, dram, sb, banks):
    with ExitStack() as own:
        def t(name, shape, dt):
            return own.enter_context(nc.sbuf_tensor(name, shape, dt))

        def sem(name):
            return own.enter_context(nc.semaphore(name))

        def two(name, shape, dt):
            return [t(f"{name}{i}", shape, dt) for i in range(2)]

        xs = [t(f"xs{i}", [P, D], F32) for i in range(XBUFS)]
        xT_hi, xT_lo = two("xT_hi", [P, KD, P], F32R), two("xT_lo", [P, KD, P], F32R)
        q_turned = t("q_turned", [P, D], F32)
        weight = t("weight", [P, BLOCKS, GROUP], F32)
        k_turned = weight[:].rearrange("p b c -> p (b c)")
        k_diag = t("k_diag", [P, BLOCKS, GROUPS, GROUP], F32)
        top, total, scale = (t(n, [P, BLOCKS], F32) for n in ("top", "total", "scale"))
        sums, sumsT = t("sums", [P, BLOCKS, 2], F32), t("sumsT", [P, 2 * HEADS], F32)
        stats, mv = two("stats", [P, 6], F32), two("mv", [P, 2], F32)
        rstd = two("rstd", [P, 1], F32)
        minus_half = t("minus_half", [P, 1], F32)
        wide = [P, ROUTE_TILES, EXPERTS]
        logits, one1, one2, tmp, rank = (t(n, wide, F32) for n in ("logits", "one1", "one2", "tmp", "rank"))
        chosen = t("chosen", wide, BF16)
        m1, m2, i1, i2 = (t(n, [P, ROUTE_TILES], F32) for n in ("m1", "m2", "i1", "i2"))
        place, number = t("place", [P, 2, ROUTE_TILES], I32), t("number", [P, ROUTE_TILES], I32)

        x_in = [sem(f"x_in{i}") for i in range(XBUFS)]
        xn_out = [sem(f"xn_out{i}") for i in range(XBUFS)]
        var_ready, rstd_ready, xn_ready = sem("var_ready"), sem("rstd_ready"), sem("xn_ready")
        turned, hi_ready, lo_ready = sem("turned"), sem("hi_ready"), sem("lo_ready")
        q_done, k_done, side_done = sem("q_done"), sem("k_done"), sem("side_done")
        qt_ready, kt_ready, k_diag_ready = sem("qt_ready"), sem("kt_ready"), sem("k_diag_ready")
        side_copied = sem("side_copied")
        scores_done, top_ready, centred, exp_ready = (sem(n) for n in ("scores_done", "top_ready", "centred", "exp_ready"))
        chosen_ready, ranks_done = sem("chosen_ready"), sem("ranks_done")
        place_ready, number_ready, scattered = sem("place_ready"), sem("number_ready"), sem("scattered")
        pool_gate, pool_consts, dve_gate = sem("pool_gate"), sem("pool_consts"), sem("dve_gate")
        dve_step = sem("route_dve_step")

        T = ROUTE_TILES
        NB = TILES // T
        BANK_X, BANK_Q, BANK_K, BANK_S, BANK_SIDE, BANK_RANK = banks[0], *banks[2:7]
        BANK_XS = banks[0:2]
        ps_rank = BANK_RANK[:, 0:T * EXPERTS]
        ps_total = BANK_RANK[:, 256:256 + EXPERTS]
        ps_values, ps_logits = BANK_SIDE[:, 0:DH], BANK_SIDE[:, DH:SIDE]

        def lagged(u, s, lag):
            return T * u + s - lag, (s - lag) % XBUFS, T // XBUFS * u + (s - lag) // XBUFS

        with nc.Block() as block:
            @block.sync
            def _(sp):
                def body(u):
                    for s in range(T):
                        i, b, before = lagged(u, s, 0)
                        if in_range(i, TILES):
                            after(sp, turned, i - XBUFS + 1)
                            after(sp, xn_out[b], 16 * before)
                            sp.dma_start(xs[b][:], dram["x_rows"][bass.ds(i * P, P), :]).then_inc(x_in[b], 16)
                        i, b, _ = lagged(u, s, 1)
                        if in_range(i, TILES):
                            sp.wait_ge(xn_ready, i + 1)
                            sp.dma_start(dram["xn_rows"][bass.ds(i * P, P), :], xs[b][:]).then_inc(xn_out[b], 16)

                turns(sp, body, 1, NB, NB + 1)
                for b in range(XBUFS):
                    sp.wait_ge(xn_out[b], 16 * TILES // XBUFS)

            @block.gpsimd
            def _(pool):
                g = nc.gpsimd
                g.memset(minus_half[:], -0.5).then_inc(pool_consts, 1)
                g.memset(k_diag[:], 0.0).then_inc(pool_consts, 1)
                pool.wait_ge(pool_consts, 1)

                def scatter(u, part):
                    if part == 0:
                        after(pool, scattered, 16 * 2 * T * u)
                        pool.sem_inc(pool_gate, 1)
                        g.tensor_copy(number[:], sb["token"][:, bass.ds(T * u, T)]).then_inc(number_ready, 1)
                        pool.wait_ge(number_ready, u + 1)
                        pool.wait_ge(place_ready, u + 1)
                        pool.sem_inc(pool_gate, 1)
                    for j in range(part * T // 4, (part + 1) * T // 4):
                        for k in range(2):
                            pool.indirect_dma_start(dram["lists"], IndirectOffsetOnAxis(place[:, k, j:j + 1], 0),
                                                    number[:, j:j + 1], None).then_inc(scattered, 16)

                def body(u):
                    for s in range(T):
                        i = T * u + s
                        if in_range(i, TILES):
                            pool.wait_ge(var_ready, i + 1)
                            g.tensor_tensor(rstd[s % 2][:], rstd[s % 2][:], minus_half[:], ALU.pow).then_inc(rstd_ready, 1)
                        if s >= 4 and in_range(u - 1, NB):
                            scatter(u - 1, s - 4)

                turns(pool, body, 2, NB, NB + 1)
                pool.wait_ge(scattered, 16 * 2 * T * NB)

            @block.scalar
            def _(act):
                a = nc.scalar
                act.wait_ge(pool_consts, 2)

                def body(u):
                    for s in range(T):
                        i, par = T * u + s - 1, (s - 1) % 2
                        if in_range(i, TILES):
                            act.wait_ge(turned, i + 1)
                            after(act, q_done, i - 1)
                            a.activation(xT_hi[par][:].rearrange("p k t -> p (k t)"), BANK_XS[par][:], ACT.Copy
                                         ).then_inc(hi_ready, 1)
                        i = T * u + s - 3
                        if in_range(i, TILES):
                            act.wait_ge(centred, i + 1)
                            a.activation(weight[:], weight[:], ACT.Exp, scale=SCORE_SCALE).then_inc(exp_ready, 1)
                        i = T * u + s - 2
                        if in_range(i, TILES):
                            act.wait_ge(kt_ready, i + 1)
                            after(act, scores_done, i)
                            for group in range(GROUPS):
                                part = slice(GROUP * group, GROUP * group + GROUP)
                                last = a.activation(k_diag[part, :, group, :],
                                                    k_turned[part, :].rearrange("p (b c) -> p b c", c=GROUP), ACT.Copy)
                            last.then_inc(k_diag_ready, 1)

                turns(act, body, 1, NB, NB + 1)

            @block.vector
            def _(dve):
                v = nc.vector
                st = Steps(dve, dve_step)

                def choose(u):
                    dve.wait_ge(side_copied, T * (u + 1))
                    st.did(v.tensor_reduce(m1[:], logits[:], AX, ALU.max)); st.wait()
                    st.did(v.tensor_tensor(tmp[:], logits[:], spread(m1[:], EXPERTS), ALU.is_equal)); st.wait()
                    st.did(v.scalar_tensor_tensor(out=tmp[:], in0=tmp[:], scalar=-float(EXPERTS), in1=sb["iota_e"][:],
                                                  op0=ALU.mult, op1=ALU.add)); st.wait()
                    st.did(v.tensor_reduce(i1[:], tmp[:], AX, ALU.min)); st.wait()
                    st.did(v.tensor_scalar(i1[:], i1[:], float(EXPERTS), None, ALU.add)); st.wait()
                    st.did(v.tensor_tensor(one1[:], sb["iota_e"][:], spread(i1[:], EXPERTS), ALU.is_equal)); st.wait()
                    st.did(v.scalar_tensor_tensor(out=logits[:], in0=one1[:], scalar=-3e38, in1=logits[:],
                                                  op0=ALU.mult, op1=ALU.add)); st.wait()
                    st.did(v.tensor_reduce(m2[:], logits[:], AX, ALU.max)); st.wait()
                    st.did(v.tensor_tensor(tmp[:], logits[:], spread(m2[:], EXPERTS), ALU.is_equal)); st.wait()
                    st.did(v.scalar_tensor_tensor(out=tmp[:], in0=tmp[:], scalar=-float(EXPERTS), in1=sb["iota_e"][:],
                                                  op0=ALU.mult, op1=ALU.add)); st.wait()
                    st.did(v.tensor_reduce(i2[:], tmp[:], AX, ALU.min)); st.wait()
                    st.did(v.tensor_scalar(i2[:], i2[:], float(EXPERTS), None, ALU.add)); st.wait()
                    st.did(v.tensor_tensor(one2[:], sb["iota_e"][:], spread(i2[:], EXPERTS), ALU.is_equal)); st.wait()
                    st.did(v.tensor_tensor(sb["gap"][:, bass.ds(T * u, T)], m2[:], m1[:], ALU.subtract))
                    v.tensor_tensor(chosen[:], one1[:], one2[:], ALU.add).then_inc(chosen_ready, 1)

                def place_tokens(u):
                    dve.wait_ge(ranks_done, u + 1)
                    st.did(v.tensor_tensor(rank[:], ps_rank.rearrange("p (t e) -> p t e", e=EXPERTS),
                                           sb["count"][:].unsqueeze(1).to_broadcast(wide), ALU.add)); st.wait()
                    st.did(v.tensor_tensor(sb["count"][:], sb["count"][:], ps_total, ALU.add))
                    after(dve, scattered, 16 * 2 * T * u)
                    for k, one in ((0, one1), (1, one2)):
                        st.did(v.tensor_tensor(tmp[:], one[:], rank[:], ALU.mult)); st.wait()
                        at = sb["pos"][:, k, bass.ds(T * u, T)]
                        st.did(v.tensor_reduce(i1[:], tmp[:], AX, ALU.add)); st.wait()
                        st.did(v.tensor_copy(at, i1[:]))
                        if k:
                            v.tensor_copy(place[:, k, :], i1[:]).then_inc(place_ready, 1)
                        else:
                            st.did(v.tensor_copy(place[:, k, :], i1[:])); st.wait()

                def body(u):
                    for s in range(T):
                        i, par = T * u + s - 1, (s - 1) % 2
                        if in_range(i, TILES):
                            dve.wait_ge(hi_ready, i + 1)
                            v.tensor_tensor(xT_lo[par][:].rearrange("p k t -> p (k t)"), BANK_XS[par][:],
                                            r32(xT_hi[par][:]).rearrange("p k t -> p (k t)"), ALU.subtract
                                            ).then_inc(lo_ready, 1)
                        i, b, before = lagged(u, s, 0)
                        par = s % 2
                        if in_range(i, TILES):
                            dve.wait_ge(x_in[b], 16 * (before + 1))
                            st.did(v.bn_stats(stats[par][:], xs[b][:])); st.wait()
                            dve.sem_inc(dve_gate, 1)
                            st.did(v.bn_aggr(mv[par][:], stats[par][:])); st.wait()
                            v.tensor_scalar(rstd[par][:], mv[par][:, 1:2], EPS, None, ALU.add).then_inc(var_ready, 1)
                        j = T * u + s - 3
                        if in_range(j, TILES):
                            dve.wait_ge(scores_done, j + 1)
                            scores = BANK_S[:].rearrange("p (b c) -> p b c", c=GROUP)
                            v.tensor_reduce(top[:], scores, AX, ALU.max).then_inc(top_ready, 1)
                            dve.wait_ge(top_ready, j + 1)
                            v.tensor_tensor(weight[:], scores, spread(top[:], GROUP), ALU.subtract).then_inc(centred, 1)
                        if in_range(i, TILES):
                            dve.wait_ge(rstd_ready, i + 1)
                            v.tensor_scalar(xs[b][:], xs[b][:], mv[par][:, 0:1], rstd[par][:, 0:1],
                                            ALU.subtract, ALU.mult).then_inc(xn_ready, 1)
                        if in_range(j, TILES):
                            dve.wait_ge(exp_ready, j + 1)
                            st.did(v.tensor_reduce(total[:], weight[:], AX, ALU.add)); st.wait()
                            st.did(v.reciprocal(scale[:], total[:])); st.wait()
                            st.did(v.tensor_tensor(total[:], total[:], scale[:], ALU.mult)); st.wait()
                            st.did(v.tensor_tensor(sums[:], spread(total[:], 2), sb["same_token"][:], ALU.mult)); st.wait()
                            st.did(v.transpose(sumsT[:], sums[:].rearrange("p b t -> p (b t)"))); st.wait()
                            st.did(v.tensor_tensor(sb["weight_sum"][:, bass.ds(j, 1), :].rearrange("p o h -> p (o h)"),
                                                   sumsT[:, 0:HEADS], sumsT[:, HEADS:], ALU.add))
                        j = T * u + s - 2
                        if in_range(j, TILES):
                            for done, bank, used, count, turned_to, ready in (
                                    (k_done, BANK_K, k_diag_ready, j, k_turned, kt_ready),
                                    (q_done, BANK_Q, scores_done, j, q_turned[:], qt_ready)):
                                if bank is BANK_Q:
                                    dve.wait_ge(side_done, j + 1)
                                    v.tensor_tensor(sb["value_sum"][:, bass.ds(j, 1), :].rearrange("p o d -> p (o d)"),
                                                    ps_values, sb["bv"][:], ALU.add)
                                    v.tensor_copy(logits[:, (s - 2) % T, :], ps_logits).then_inc(side_copied, 1)
                                dve.wait_ge(done, j + 1)
                                after(dve, used, count)
                                v.transpose(turned_to.rearrange("p (t h) -> p h t", h=HEADS),
                                            bank[:].rearrange("p (h d) -> p h d", h=HEADS)).then_inc(ready, 1)
                        if in_range(u - 1, NB):
                            if s == 1:
                                choose(u - 1)
                            if s == 3:
                                place_tokens(u - 1)

                st.turns(body, 2, NB, NB + 1, 8 * T + 14 + 9)

            @block.tensor
            def _(pe):
                m = nc.tensor

                def product(out, par, weights_hi, weights_lo, start):
                    for k in range(KD):
                        m.matmul(out, xT_hi[par][:, k, :], weights_hi[:, k, :], start=start and k == 0, stop=False)
                        m.matmul(out, xT_hi[par][:, k, :], weights_lo[:, k, :], start=False, stop=False)
                        last = m.matmul(out, xT_lo[par][:, k, :], weights_hi[:, k, :], start=False, stop=k == KD - 1)
                    return last

                def ranks(u):
                    pe.wait_ge(chosen_ready, u + 1)
                    ch = chosen[:].rearrange("p t e -> p (t e)")
                    n = T * EXPERTS
                    m.matmul(ps_rank, sb["below"][:], ch, start=True, stop=False)
                    for d in range(1, T):
                        m.matmul(ps_rank[:, EXPERTS * d:n], sb["ones_bf"][:], ch[:, 0:n - EXPERTS * d],
                                 start=False, stop=d == T - 1)
                    for d in range(T):
                        last = m.matmul(ps_total, sb["ones_bf"][:], ch[:, EXPERTS * d:EXPERTS * d + EXPERTS],
                                        start=d == 0, stop=d == T - 1)
                    last.then_inc(ranks_done, 1)

                def body(u):
                    for s in range(T):
                        i, b, _ = lagged(u, s, 1)
                        par = (s - 1) % 2
                        if in_range(i, TILES):
                            pe.wait_ge(xn_ready, i + 1)
                            after(pe, lo_ready, i - 1)
                            for k in range(KD):
                                last = m.transpose(BANK_XS[par][:, P * k:P * k + P], xs[b][:, P * k:P * k + P],
                                                   sb["ident"][:])
                            last.then_inc(turned, 1)
                        j = T * u + s - 3
                        if in_range(j, TILES):
                            pe.wait_ge(k_diag_ready, j + 1)
                            pe.wait_ge(qt_ready, j + 1)
                            after(pe, centred, j)
                            m.matmul(BANK_S[:], sb["ident_bf"][:], sb["mask"][:].rearrange("p b c -> p (b c)"),
                                     start=True, stop=False)
                            for b in range(BLOCKS):
                                c, strip = b // GROUPS, slice(GROUP * (b % GROUPS), GROUP * (b % GROUPS) + GROUP)
                                last = m.matmul(BANK_S[strip, P * c:P * c + P], q_turned[:, GROUP * b:GROUP * b + GROUP],
                                                k_diag[:, b].rearrange("p g c -> p (g c)"),
                                                start=False, stop=c == BLOCKS // GROUPS - 1)
                            last.then_inc(scores_done, 1)
                        j, par = T * u + s - 2, s % 2
                        if in_range(j, TILES):
                            pe.wait_ge(hi_ready, j + 1)
                            pe.wait_ge(lo_ready, j + 1)
                            for n, bank, w, done, copied in ((1, BANK_K, "wk", k_done, kt_ready),
                                                             (0, BANK_Q, "proj", q_done, qt_ready)):
                                if n == 0:
                                    after(pe, side_copied, j)
                                    product(BANK_SIDE[:, 0:SIDE], par, sb["side_hi"], sb["side_lo"], True
                                            ).then_inc(side_done, 1)
                                after(pe, copied, j)
                                add_bias(bank, sb, m, n)
                                product(bank[:], par, sb[w + "_hi"], sb[w + "_lo"], False).then_inc(done, 1)
                        if s == 2 and in_range(u - 1, NB):
                            ranks(u - 1)

                turns(pe, body, 1, NB, NB + 1)


def experts(nc, dram, sb, banks):
    with ExitStack() as own:
        def t(name, shape, dt):
            return own.enter_context(nc.sbuf_tensor(name, shape, dt))

        def sem(name):
            return own.enter_context(nc.semaphore(name))

        def two(name, shape, dt):
            return [t(f"{name}{i}", shape, dt) for i in range(2)]

        wide = [P, SLOT_TILES, EXPERTS]
        tile_no = t("tile_no", [P, SLOT_TILES], F32)
        expert_no, pick = t("expert_no", wide, F32), t("pick", wide, F32)
        need_i, need = t("need_i", [P, EXPERTS], I32), t("need", [P, EXPERTS], F32)
        ones8, end = t("ones8", [P, EXPERTS], F32), t("end", [P, EXPERTS], F32)
        start, shift = t("start", [P, EXPERTS], F32), t("shift", [P, EXPERTS], F32)
        step_to = t("step_to", [P, EXPERTS], F32)
        of_tile, begin = t("of_tile", [P, SLOT_TILES], F32), t("begin", [P, SLOT_TILES], F32)
        three = t("three", [P, SLOT_TILES // 2 + 1], F32)
        experts_of, row_of = t("experts_of", [P, SLOT_TILES // 2 + 1], I32), t("row_of", [P, SLOT_TILES], I32)
        half_inv, half_inv2 = t("half_inv", [P, SLOT_TILES], F32), t("half_inv2", [P, SLOT_TILES], F32)

        rows = two("rows", [P, 1], I32)
        xg = two("xg", [P, D], F32)
        xT_hi, xT_lo = two("xgT_hi", [P, KD, P], F16), two("xgT_lo", [P, KD, P], F16)
        th, gated, inter = two("th", [P, FF], F32), two("gated", [P, FF], F32), two("inter", [P, FF], F32)
        iT_hi, iT_lo = two("iT_hi", [P, KF, P], F32R), two("iT_lo", [P, KF, P], F32R)
        out = two("e_out", [P, D], F32)

        wout_raw = t("wout_raw", [P, KD, D], F32)
        wout_in, wout_hi_ready = sem("wout_in"), sem("wout_hi_ready")
        numbers = sem("numbers")
        tables_ready = sem("tables_ready")
        rows_in = [sem("rows_in0"), sem("rows_in1")]
        gathered = [sem("gathered0"), sem("gathered1")]
        stored = [sem("e_stored0"), sem("e_stored1")]
        turned, hi_ready, lo_ready = sem("e_turned"), sem("e_hi_ready"), sem("e_lo_ready")
        up_done, th_ready, inter_ready = sem("up_done"), sem("th_ready"), sem("inter_ready")
        iturned, ihi_ready, ilo_ready = sem("iturned"), sem("ihi_ready"), sem("ilo_ready")
        down_done, out_ready = sem("down_done"), sem("out_ready")
        sp_gate = sem("e_sp_gate")
        pool_gate, gated_ready, dve_step = sem("e_pool_gate"), sem("gated_ready"), sem("e_dve_step")

        N = SLOT_TILES
        FIRST, LAST, LAG = 3, N // 2, 6
        END = (N + LAG) // 2 + 1

        def body_of(step):
            def body(u):
                for s in range(2):
                    step(2 * u + s, u, s)
            return body

        with nc.Block() as block:
            @block.sync
            def _(sp):
                sp.dma_start(wout_raw[:], dram["wout"].rearrange("(k p) n -> p k n", p=P)).then_inc(wout_in, 16)
                sp.wait_ge(tables_ready, 1)

                def step(j, u, s):
                    if in_range(j, N):
                        after(sp, gathered[s], 16 * u)
                        sp.sem_inc(sp_gate, 1)
                        at = sp.value_load(row_of[0:1, bass.ds(j, 1)], min_val=0, max_val=EXPERTS * REGION - P)
                        sp.dma_start(rows[s][:], dram["lists"][bass.ds(at, P), :]).then_inc(rows_in[s], 16)
                    i = j - LAG
                    if in_range(i, N):
                        sp.wait_ge(out_ready, i + 1)
                        sp.dma_start(dram["expert_rows"][bass.ds(i * P, P), :], out[s][:]).then_inc(stored[s], 16)

                turns(sp, body_of(step), FIRST, LAST, END)
                for s in range(2):
                    sp.wait_ge(stored[s], 16 * N // 2)

            @block.gpsimd
            def _(pool):
                g = nc.gpsimd
                g.iota(tile_no[:], pattern=[[1, N]], base=0, channel_multiplier=0,
                       allow_small_or_imprecise_dtypes=True).then_inc(numbers, 1)
                g.iota(expert_no[:], pattern=[[0, N], [1, EXPERTS]], base=0, channel_multiplier=0,
                       allow_small_or_imprecise_dtypes=True).then_inc(numbers, 1)
                g.memset(ones8[:], 1.0).then_inc(numbers, 1)

                def step(j, u, s):
                    if in_range(j, N):
                        after(pool, turned, j - 1)
                        pool.wait_ge(rows_in[s], 16 * (u + 1))
                        pool.sem_inc(pool_gate, 1)
                        pool.indirect_dma_start(xg[s][:], None, dram["xn_rows"],
                                                IndirectOffsetOnAxis(rows[s][:, 0:1], 0)).then_inc(gathered[s], 16)

                turns(pool, body_of(step), FIRST, LAST, LAST)

            @block.scalar
            def _(act):
                a = nc.scalar
                act.wait_ge(wout_in, 16)
                a.activation(sb["proj_hi"][:], wout_raw[:], ACT.Copy).then_inc(wout_hi_ready, 1)
                act.wait_ge(tables_ready, 1)

                def step(j, u, s):
                    if in_range(j, N):
                        act.wait_ge(turned, j + 1)
                        after(act, up_done, j - 1)
                        a.activation(xT_hi[s][:].rearrange("p k t -> p (k t)"), banks[s][:], ACT.Copy
                                     ).then_inc(hi_ready, 1)
                    i = j - 2
                    if in_range(i, N):
                        act.wait_ge(iturned, i + 1)
                        after(act, down_done, i - 1)
                        a.activation(iT_hi[s][:].rearrange("p k t -> p (k t)"), banks[4 + s][:, 0:FF], ACT.Copy
                                     ).then_inc(ihi_ready, 1)
                    i, o = j - 3, 1 - s
                    if in_range(i, N):
                        act.wait_ge(down_done, i + 1)
                        after(act, stored[o], 16 * (u - 2 + s))
                        a.activation(out[o][:], banks[6 + o][:], ACT.Copy).then_inc(out_ready, 1)
                    i = j - 1
                    if in_range(i, N):
                        act.wait_ge(up_done, i + 1)
                        after(act, gated_ready, i - 1)
                        a.activation(th[o][:], banks[2 + o][:, 0:FF], ACT.Tanh,
                                     scale=half_inv[:, bass.ds(i, 1)]).then_inc(th_ready, 1)

                turns(act, body_of(step), FIRST, LAST, END)

            @block.vector
            def _(dve):
                v = nc.vector
                st = Steps(dve, dve_step)

                def per_tile(ap):
                    return ap.unsqueeze(1).to_broadcast(wide)

                dve.wait_ge(numbers, 3)
                st.did(v.scalar_tensor_tensor(out=need_i[:], in0=sb["count"][:], scalar=float(P - 1),
                                              in1=sb["region"][:], op0=ALU.add, op1=ALU.subtract)); st.wait()
                st.did(v.tensor_scalar(need_i[:], need_i[:], P.bit_length() - 1, None, ALU.arith_shift_right)); st.wait()
                st.did(v.tensor_copy(need[:], need_i[:])); st.wait()
                st.did(v.tensor_tensor_scan(end[:], ones8[:], need[:], 0.0, ALU.mult, ALU.add)); st.wait()
                st.did(v.tensor_tensor(start[:], end[:], need[:], ALU.subtract)); st.wait()
                st.did(v.tensor_tensor(pick[:], spread(tile_no[:], EXPERTS), per_tile(end[:]), ALU.is_ge)); st.wait()
                st.did(v.tensor_reduce(of_tile[:], pick[:], AX, ALU.add)); st.wait()
                st.did(v.tensor_scalar(of_tile[:], of_tile[:], float(EXPERTS - 1), None, ALU.min)); st.wait()
                pairs = of_tile[:].rearrange("p (u t) -> p u t", t=2)
                st.did(v.memset(three[:], 0.0)); st.wait()
                st.did(v.tensor_copy(three[:, 1:], pairs[:, :, 0])); st.wait()
                st.did(v.scalar_tensor_tensor(out=three[:, 1:], in0=pairs[:, :, 1], scalar=float(EXPERTS),
                                              in1=three[:, 1:], op0=ALU.mult, op1=ALU.add)); st.wait()
                st.did(v.scalar_tensor_tensor(out=three[:, 0:N // 2], in0=pairs[:, :, 0], scalar=float(EXPERTS ** 2),
                                              in1=three[:, 0:N // 2], op0=ALU.mult, op1=ALU.add)); st.wait()
                st.did(v.tensor_copy(experts_of[:], three[:]))
                st.did(v.tensor_tensor(expert_no[:], expert_no[:], spread(of_tile[:], EXPERTS), ALU.is_equal)); st.wait()
                st.did(v.tensor_tensor(pick[:], expert_no[:], per_tile(start[:]), ALU.mult)); st.wait()
                st.did(v.tensor_reduce(begin[:], pick[:], AX, ALU.add)); st.wait()
                st.did(v.tensor_tensor(begin[:], tile_no[:], begin[:], ALU.subtract)); st.wait()
                st.did(v.tensor_scalar(begin[:], begin[:], float(REGION // P - 1), float(P), ALU.min, ALU.mult)); st.wait()
                st.did(v.scalar_tensor_tensor(out=row_of[:], in0=of_tile[:], scalar=float(REGION), in1=begin[:],
                                              op0=ALU.mult, op1=ALU.add))
                st.did(v.tensor_tensor(pick[:], expert_no[:], per_tile(sb["wi_inv"][:]), ALU.mult)); st.wait()
                st.did(v.tensor_reduce(begin[:], pick[:], AX, ALU.add)); st.wait()
                st.did(v.tensor_scalar(half_inv[:], begin[:], 0.5, None, ALU.mult)); st.wait()
                st.did(v.tensor_tensor(half_inv2[:], half_inv[:], begin[:], ALU.mult)); st.wait()
                dve.sem_inc(tables_ready, 1)
                st.did(v.scalar_tensor_tensor(out=shift[:], in0=start[:], scalar=float(P), in1=sb["region"][:],
                                              op0=ALU.mult, op1=ALU.subtract)); st.wait()
                st.did(v.tensor_copy(step_to[:, 0:1], shift[:, 0:1]))
                st.did(v.tensor_tensor(step_to[:, 1:], shift[:, 1:], shift[:, 0:EXPERTS - 1], ALU.subtract)); st.wait()
                for k in range(2):
                    part = pick[:, 0:TILES, :]
                    many = [P, TILES, EXPERTS]
                    st.did(v.tensor_tensor(part, spread(sb["pos"][:, k, :], EXPERTS),
                                           sb["region"][:].unsqueeze(1).to_broadcast(many), ALU.is_ge)); st.wait()
                    st.did(v.tensor_tensor(part, part, step_to[:].unsqueeze(1).to_broadcast(many), ALU.mult)); st.wait()
                    st.did(v.tensor_reduce(begin[:, 0:TILES], part, AX, ALU.add)); st.wait()
                    st.did(v.tensor_tensor(sb["slot"][:, k, :], begin[:, 0:TILES], sb["pos"][:, k, :], ALU.add)); st.wait()
                dve.wait_ge(wout_hi_ready, 1)
                v.tensor_tensor(sb["proj_lo"][:], wout_raw[:], r32(sb["proj_hi"][:]), ALU.subtract)

                def step(j, u, s):
                    if in_range(j, N):
                        dve.wait_ge(hi_ready, j + 1)
                        v.tensor_tensor(xT_lo[s][:].rearrange("p k t -> p (k t)"), banks[s][:],
                                        xT_hi[s][:].rearrange("p k t -> p (k t)"), ALU.subtract).then_inc(lo_ready, 1)
                    i = j - 2
                    if in_range(i, N):
                        dve.wait_ge(ihi_ready, i + 1)
                        v.tensor_tensor(iT_lo[s][:].rearrange("p k t -> p (k t)"), banks[4 + s][:, 0:FF],
                                        r32(iT_hi[s][:]).rearrange("p k t -> p (k t)"), ALU.subtract
                                        ).then_inc(ilo_ready, 1)
                    i, o = j - 1, 1 - s
                    if in_range(i, N):
                        dve.wait_ge(th_ready, i + 1)
                        v.scalar_tensor_tensor(out=gated[o][:], in0=th[o][:], scalar=1.0, in1=banks[2 + o][:, 0:FF],
                                               op0=ALU.add, op1=ALU.mult).then_inc(gated_ready, 1)
                        dve.wait_ge(gated_ready, i + 1)
                        after(dve, iturned, i - 1)
                        v.scalar_tensor_tensor(out=inter[o][:], in0=banks[2 + o][:, FF:2 * FF],
                                               scalar=half_inv2[:, bass.ds(i, 1)], in1=gated[o][:],
                                               op0=ALU.mult, op1=ALU.mult).then_inc(inter_ready, 1)

                turns(dve, body_of(step), FIRST, LAST, END)

            @block.tensor
            def _(pe):
                m = nc.tensor
                pe.wait_ge(tables_ready, 1)

                def load_experts(u):
                    three = pe.value_load(experts_of[0:1, bass.ds(u, 1)], min_val=0, max_val=EXPERTS ** 3 - 1)
                    return three % EXPERTS, three // EXPERTS % EXPERTS, three // EXPERTS ** 2

                def weights(name, e, k):
                    return sb[name][:, bass.ds(e, 1), k, :].rearrange("p o n -> p (o n)")

                def up(i, o, e, chunks):
                    for k in chunks:
                        m.matmul(banks[2 + o][:], xT_hi[o][:, k, :], weights("wi_hi", e, k), start=k == 0, stop=False)
                        m.matmul(banks[2 + o][:], xT_hi[o][:, k, :], weights("wi_lo", e, k), start=False, stop=False)
                        last = m.matmul(banks[2 + o][:], xT_lo[o][:, k, :], weights("wi_hi", e, k), start=False,
                                        stop=k == KD - 1)
                    return last

                def body(u):
                    e = load_experts(u) if in_range(u, N // 2 + 1) else (None,) * 3
                    for s in range(2):
                        step(2 * u + s, u, s, e[s + 1], e[s])

                def step(j, u, s, e_up, e_down):
                    o = 1 - s
                    if in_range(j, N):
                        pe.wait_ge(gathered[s], 16 * (u + 1))
                        after(pe, lo_ready, j - 1)
                        for k in range(KD):
                            last = m.transpose(banks[s][:, P * k:P * k + P], xg[s][:, P * k:P * k + P], sb["ident"][:])
                        last.then_inc(turned, 1)
                    i = j - 1
                    if in_range(i, N):
                        pe.wait_ge(hi_ready, i + 1)
                        pe.wait_ge(lo_ready, i + 1)
                        after(pe, inter_ready, i - 1)
                        up(i, o, e_up, range(KD // 2))
                    i = j - 2
                    if in_range(i, N):
                        pe.wait_ge(inter_ready, i + 1)
                        after(pe, ilo_ready, i - 1)
                        for k in range(KF):
                            last = m.transpose(banks[4 + s][:, P * k:P * k + P], inter[s][:, P * k:P * k + P],
                                               sb["ident"][:])
                        last.then_inc(iturned, 1)
                    i = j - 1
                    if in_range(i, N):
                        up(i, o, e_up, range(KD // 2, KD)).then_inc(up_done, 1)
                    i = j - 2
                    if in_range(i, N):
                        pe.wait_ge(ihi_ready, i + 1)
                        pe.wait_ge(ilo_ready, i + 1)
                        after(pe, out_ready, i - 1)
                        for k in range(KF):
                            m.matmul(banks[6 + s][:], iT_hi[s][:, k, :], weights("wo_hi", e_down, k), start=k == 0,
                                     stop=False)
                            m.matmul(banks[6 + s][:], iT_hi[s][:, k, :], weights("wo_lo", e_down, k), start=False,
                                     stop=False)
                            last = m.matmul(banks[6 + s][:], iT_lo[s][:, k, :], weights("wo_hi", e_down, k), start=False,
                                            stop=k == KF - 1)
                        last.then_inc(down_done, 1)

                turns(pe, body, FIRST, LAST, END)


def combine(nc, dram, sb, banks):
    with ExitStack() as own:
        def t(name, shape, dt):
            return own.enter_context(nc.sbuf_tensor(name, shape, dt))

        def sem(name):
            return own.enter_context(nc.semaphore(name))

        def four(name, shape, dt):
            return [t(f"{name}{i}", shape, dt) for i in range(4)]

        w1, w2, ew = (t(n, [P, TILES], F32) for n in ("w1", "w2", "ew"))
        heads = four("heads", [P, HEADS, DH], F32)
        hT_hi, hT_lo = four("hT_hi", [P, HC, P], F32R), four("hT_lo", [P, HC, P], F32R)
        idx, ya, yb = four("idx", [P, 2], I32), four("ya", [P, D], F32), four("yb", [P, D], F32)
        part, mixed, th, gate = (four(n, [P, D], F32) for n in ("part", "mixed", "g_th", "gate"))
        x_in, gated, final = four("xr", [P, D], F32), four("y_gated", [P, D], F32), four("final", [P, D], F32)

        turn_rows = t("turn_rows", [P, P], F32)
        weight_sum = t("weight_sum_ordered", [P, TILES, HEADS], F32)

        wts, order_ready, ordered, order_copied = sem("wts"), sem("order_ready"), sem("ordered"), sem("order_copied")
        x_got = [sem(f"x_got{i}") for i in range(4)]
        fetched = [sem(f"fetched{i}") for i in range(4)]
        stored = [sem(f"f_stored{i}") for i in range(4)]
        heads_ready, h_turned, hT_hi_ready, hT_lo_ready = (
            sem(n) for n in ("heads_ready", "h_turned", "hT_hi_ready", "hT_lo_ready"))
        idx_ready, pool_gate, dve_gate = sem("idx_ready"), sem("c_pool_gate"), sem("c_dve_gate")
        part_ready, mixed_ready, th_ready, gate_ready = (
            sem(n) for n in ("part_ready", "mixed_ready", "c_th_ready", "gate_ready"))
        y_done, gated_ready, final_ready = sem("y_done"), sem("c_gated_ready"), sem("final_ready")

        N = TILES
        FIRST, LAST, LAG = 3, N // 4, 8
        END = (N + LAG) // 4
        BANK_H, BANK_Y = banks[0:4], banks[4:8]

        def body_of(step):
            def body(u):
                for s in range(4):
                    step(lambda lag: (4 * u + s - lag, (s - lag) % 4, u + (s - lag) // 4))
            return body

        with nc.Block() as block:
            @block.sync
            def _(sp):
                def step(at):
                    j, b, _ = at(3)
                    if in_range(j, N):
                        after(sp, final_ready, j - 3)
                        sp.dma_start(x_in[b][:], dram["x_rows"][bass.ds(j * P, P), :]).then_inc(x_got[b], 16)
                    j, b, _ = at(6)
                    if in_range(j, N):
                        sp.wait_ge(final_ready, j + 1)
                        sp.dma_start(dram["out"][bass.ds(j * P, P), :], final[b][:]).then_inc(stored[b], 16)

                turns(sp, body_of(step), FIRST, LAST, END)
                for b in range(4):
                    sp.wait_ge(stored[b], 16 * N // 4)

            @block.gpsimd
            def _(pool):
                g = nc.gpsimd
                to = turn_rows[:].rearrange("p (g c j t) -> p g c j t", g=GROUPS, c=GROUPS, t=2)
                frm = sb["ident"][:].rearrange("p (j c g t) -> p g c j t", g=GROUPS, c=GROUPS, t=2)
                for i in range(GROUPS):
                    g.tensor_copy(to[:, i], frm[:, i]).then_inc(order_ready, 1)

                def step(at):
                    j, b, before = at(0)
                    if in_range(j, N):
                        after(pool, fetched[b], 32 * before)
                        after(pool, mixed_ready, j - 3)
                        pool.sem_inc(pool_gate, 1)
                        g.tensor_copy(idx[b][:], sb["slot"][:, :, bass.ds(j, 1)].rearrange("p k o -> p (k o)")
                                      ).then_inc(idx_ready, 1)
                        pool.wait_ge(idx_ready, j + 1)
                        pool.sem_inc(pool_gate, 1)
                        for k, to in ((0, ya[b]), (1, yb[b])):
                            pool.indirect_dma_start(to[:], None, dram["expert_rows"],
                                                    IndirectOffsetOnAxis(idx[b][:, k:k + 1], 0)
                                                    ).then_inc(fetched[b], 16)
                    j, b, before = at(5)
                    if in_range(j, N):
                        pool.wait_ge(gated_ready, j + 1)
                        pool.wait_ge(x_got[b], 16 * (before + 1))
                        after(pool, stored[b], 16 * before)
                        pool.sem_inc(pool_gate, 1)
                        g.tensor_tensor(final[b][:], gated[b][:], x_in[b][:], ALU.add).then_inc(final_ready, 1)

                turns(pool, body_of(step), FIRST, LAST, END)

            @block.scalar
            def _(act):
                a = nc.scalar
                a.activation(ew[:], sb["gap"][:], ACT.Exp).then_inc(wts, 1)
                act.wait_ge(wts, 4)

                def step(at):
                    j, b, _ = at(1)
                    if in_range(j, N):
                        act.wait_ge(h_turned, j + 1)
                        after(act, y_done, j - 3)
                        a.activation(hT_hi[b][:].rearrange("p c t -> p (c t)"), BANK_H[b][:], ACT.Copy
                                     ).then_inc(hT_hi_ready, 1)
                    j, b, before = at(2)
                    if in_range(j, N):
                        act.wait_ge(fetched[b], 32 * (before + 1))
                        after(act, mixed_ready, j - 3)
                        a.activation(part[b][:], ya[b][:], ACT.Copy, scale=w1[:, bass.ds(j, 1)]).then_inc(part_ready, 1)
                    j, b, _ = at(3)
                    if in_range(j, N):
                        act.wait_ge(mixed_ready, j + 1)
                        after(act, gate_ready, j - 3)
                        a.activation(th[b][:], mixed[b][:], ACT.Tanh, scale=0.5).then_inc(th_ready, 1)

                turns(act, body_of(step), FIRST, LAST, END)

            @block.vector
            def _(dve):
                v = nc.vector
                dve.wait_ge(wts, 1)
                v.tensor_scalar(w2[:], ew[:], 1.0, None, ALU.add).then_inc(wts, 1)
                dve.wait_ge(wts, 2)
                v.reciprocal(w1[:], w2[:]).then_inc(wts, 1)
                dve.wait_ge(wts, 3)
                v.tensor_tensor(w2[:], ew[:], w1[:], ALU.mult).then_inc(wts, 1)
                dve.wait_ge(wts, 4)
                dve.wait_ge(ordered, 1)
                for n in range(2):
                    half = slice(TILES // 2 * n, TILES // 2 * (n + 1))
                    v.tensor_copy(weight_sum[:, half, :].rearrange("p i h -> p (i h)"), BANK_Y[n][:]
                                  ).then_inc(order_copied, 1)
                dve.wait_ge(order_copied, 2)

                def step(at):
                    j, b, _ = at(0)
                    if in_range(j, N):
                        after(dve, h_turned, j - 3)
                        v.tensor_tensor(heads[b][:], spread(weight_sum[:, bass.ds(j, 1), :].rearrange(
                                            "p o h -> p (o h)"), DH),
                                        sb["value_sum"][:, bass.ds(j, 1), :].to_broadcast([P, HEADS, DH]), ALU.mult
                                        ).then_inc(heads_ready, 1)
                    j, b, _ = at(2)
                    if in_range(j, N):
                        dve.wait_ge(part_ready, j + 1)
                        after(dve, gate_ready, j - 3)
                        v.scalar_tensor_tensor(out=mixed[b][:], in0=yb[b][:], scalar=w2[:, bass.ds(j, 1)],
                                               in1=part[b][:], op0=ALU.mult, op1=ALU.add).then_inc(mixed_ready, 1)
                    j, b, _ = at(1)
                    if in_range(j, N):
                        dve.wait_ge(hT_hi_ready, j + 1)
                        after(dve, y_done, j - 3)
                        v.tensor_tensor(hT_lo[b][:].rearrange("p c t -> p (c t)"), BANK_H[b][:],
                                        r32(hT_hi[b][:]).rearrange("p c t -> p (c t)"), ALU.subtract
                                        ).then_inc(hT_lo_ready, 1)
                    j, b, _ = at(3)
                    if in_range(j, N):
                        dve.wait_ge(th_ready, j + 1)
                        v.scalar_tensor_tensor(out=gate[b][:], in0=th[b][:], scalar=1.0, in1=mixed[b][:],
                                               op0=ALU.add, op1=ALU.mult).then_inc(gate_ready, 1)
                    j, b, _ = at(4)
                    if in_range(j, N):
                        dve.wait_ge(y_done, j + 1)
                        after(dve, final_ready, j - 3)
                        dve.wait_ge(gate_ready, j + 1)
                        v.scalar_tensor_tensor(out=gated[b][:], in0=BANK_Y[b][:], scalar=0.5, in1=gate[b][:],
                                               op0=ALU.mult, op1=ALU.mult).then_inc(gated_ready, 1)

                turns(dve, body_of(step), FIRST, LAST, END)

            @block.tensor
            def _(pe):
                m = nc.tensor
                pe.wait_ge(order_ready, GROUPS)
                for n in range(2):
                    half = slice(TILES // 2 * n, TILES // 2 * (n + 1))
                    last = m.matmul(BANK_Y[n][:], turn_rows[:], sb["weight_sum"][:, half, :].rearrange("p i h -> p (i h)"),
                                    start=True, stop=True)
                last.then_inc(ordered, 1)
                pe.wait_ge(order_copied, 2)

                def step(at):
                    j, b, _ = at(1)
                    if in_range(j, N):
                        pe.wait_ge(heads_ready, j + 1)
                        after(pe, hT_lo_ready, j - 3)
                        for c in range(HC):
                            last = m.transpose(BANK_H[b][:, P * c:P * c + P],
                                               heads[b][:].rearrange("p h d -> p (h d)")[:, P * c:P * c + P],
                                               sb["ident"][:])
                        last.then_inc(h_turned, 1)
                    j, b, _ = at(2)
                    if in_range(j, N):
                        pe.wait_ge(hT_hi_ready, j + 1)
                        pe.wait_ge(hT_lo_ready, j + 1)
                        after(pe, gated_ready, j - 3)
                        out, w_hi, w_lo = BANK_Y[b], sb["proj_hi"][:], sb["proj_lo"][:]
                        add_bias(out, sb, m, 2)
                        for c in range(HC):
                            m.matmul(out[:], hT_hi[b][:, c, :], w_hi[:, c, :], start=False, stop=False)
                            m.matmul(out[:], hT_hi[b][:, c, :], w_lo[:, c, :], start=False, stop=False)
                            last = m.matmul(out[:], hT_lo[b][:, c, :], w_hi[:, c, :], start=False, stop=c == HC - 1)
                        last.then_inc(y_done, 1)

                turns(pe, body_of(step), FIRST, LAST, END)


def build(nc, dram):
    ctx = ExitStack()
    with ctx:
        def t(name, shape, dt):
            return ctx.enter_context(nc.sbuf_tensor(name, shape, dt))

        sb = {
            "proj_hi": t("proj_hi", [P, KD, D], F32R), "proj_lo": t("proj_lo", [P, KD, D], F32R),
            "side_hi": t("side_hi", [P, KD, SIDE], F32R), "side_lo": t("side_lo", [P, KD, SIDE], F32R),
            "biases": t("biases", [P, D], F32R), "bv": t("bv_sum", [P, DH], F32),
            "same_token": t("same_token", [P, BLOCKS, 2], F32),
            "weight_sum": t("weight_sum", [P, TILES, HEADS], F32), "value_sum": t("value_sum", [P, TILES, DH], F32),
            "ones_r": t("ones_r", [P, P], F32R),
            "ident": t("ident", [P, P], F32), "ident_bf": t("ident_bf", [P, P], BF16),
            "below": t("below", [P, P], BF16), "ones_bf": t("ones_bf", [P, P], BF16),
            "mask": t("mask", [P, BLOCKS, 2 * HEADS], BF16),
            "token": t("token", [P, TILES], I32),
            "iota_e": t("iota_e", [P, ROUTE_TILES, EXPERTS], F32),
            "count": t("count", [P, EXPERTS], F32), "region": t("region", [P, EXPERTS], F32),
            "wi_scale": t("wi_scale", [P, EXPERTS], F32), "wi_inv": t("wi_inv", [P, EXPERTS], F32),
            "gap": t("gap", [P, TILES], F32), "pos": t("pos", [P, 2, TILES], F32),
            "slot": t("slot", [P, 2, TILES], I32),
        }
        psum = ctx.enter_context(nc.psum_tensor("psum", [P, 8, 512], F32))
        banks = [psum[:, i, :] for i in range(8)]
        dram = dict(dram)
        for name, shape, dt in (
            ("xn_rows", [TOKENS, D], F32),
            ("lists", [EXPERTS * REGION, 1], I32), ("expert_rows", [SLOT_TILES * P, D], F32),
        ):
            dram[name] = nc.dram_tensor(name + "_scratch", shape, dt).ap()
        with ExitStack() as weights:
            def w(name, shape, dt):
                return weights.enter_context(nc.sbuf_tensor(name, shape, dt))

            sb |= {
                "wi_hi": w("wi_hi", [P, EXPERTS, KD, 2 * FF], F16), "wi_lo": w("wi_lo", [P, EXPERTS, KD, 2 * FF], F16),
                "wo_hi": w("wo_hi", [P, EXPERTS, KF, D], F32R), "wo_lo": w("wo_lo", [P, EXPERTS, KF, D], F32R),
            }
            with ExitStack() as keys:
                for part in ("hi", "lo"):
                    sb["wk_" + part] = keys.enter_context(nc.sbuf_tensor("wk_" + part, [P, KD, D], F32R))
                prepare(nc, dram, sb, banks)
                attend_and_route(nc, dram, sb, banks)
            experts(nc, dram, sb, banks)
        combine(nc, dram, sb, banks)


def kernel(**inputs):
    import concourse.bacc as bacc
    from concourse.bass_utils import run_bass_kernel_spmd

    a = {k: np.asarray(v) for k, v in inputs.items()}
    w = a["L0_attn_Wqkv"]
    b = a["L0_attn_bqkv"]
    arrays = {
        "x_rows": a["L0_attn_x"].reshape(TOKENS, D),
        "wq": w[:, :, 0:DH].reshape(D, HEADS * DH), "wk": w[:, :, DH:2 * DH].reshape(D, HEADS * DH),
        "wv": w[:, :, 2 * DH:].reshape(D, HEADS * DH),
        "biases": np.stack([b[:, 0:DH].reshape(-1), b[:, DH:2 * DH].reshape(-1), a["L0_attn_bout"],
                            b[:, 2 * DH:].reshape(-1)]),
        "wout": a["L0_attn_Wout"].reshape(HEADS * DH, D),
        "w_gate": a["L0_ffn_w_gate"], "wi_0": a["L0_ffn_wi_0"], "wi_1": a["L0_ffn_wi_1"], "wo": a["L0_ffn_wo"],
    }
    nc = bacc.Bacc("TRN2", target_bir_lowering=False, num_devices=1)
    dram = {}
    for name in list(arrays):
        arrays["in_" + name] = np.ascontiguousarray(arrays.pop(name))
        dram[name] = nc.dram_tensor("in_" + name, arrays["in_" + name].shape, F32, kind="ExternalInput").ap()
    dram["out"] = nc.dram_tensor("out", [TOKENS, D], F32, kind="ExternalOutput").ap()
    build(nc, dram)
    r = run_bass_kernel_spmd(nc, [arrays], core_ids=[0])
    return np.asarray(r.results[0]["out"]).reshape(BATCH, SEQ, D)
```

```python
from contextlib import ExitStack

import concourse.bass as bass
import concourse.mybir as mybir
import numpy as np
from concourse.bass import IndirectOffsetOnAxis

F32, F32R, F16, BF16, I32 = (mybir.dt.float32, mybir.dt.float32r, mybir.dt.float16, mybir.dt.bfloat16,
                             mybir.dt.int32)
ALU = mybir.AluOpType
ACT = mybir.ActivationFunctionType
AX = mybir.AxisListType.X
REDUCE_MAX = bass.bass_isa.ReduceOp.max

P = 128
BATCH, SEQ, D = 2, 4096, 512
TOKENS = BATCH * SEQ
HEADS, DH = 16, 32
EXPERTS, TOPK, FF = 8, 2, 256
KD = D // P
KF = FF // P
HC = HEADS * DH // P
TILES = TOKENS // P
SLOT_TILES = TOKENS * TOPK // P + EXPERTS
REGION = TOKENS
EPS = 1e-5
GROUP = 32
GROUPS = P // GROUP
BLOCKS = P // (GROUPS * 2)
ROUTE_TILES = 8
XBUFS = 2
SIDE = DH + EXPERTS
MASKED = -1e9 * float(np.sqrt(DH))
SCORE_SCALE = 1.0 / float(np.sqrt(DH))
EXPONENT = 0x7F800000
SMALLEST = 2.0 ** -40


def after(eng, sem, n):
    if not isinstance(n, int) or n > 0:
        eng.wait_ge(sem, n)


def in_range(i, n):
    return not isinstance(i, int) or 0 <= i < n


def turns(eng, body, first, last, end):
    for u in range(first):
        body(u)
    with eng.Fori(first, last) as u:
        body(u)
    for u in range(last, end):
        body(u)


class Steps:

    def __init__(self, eng, sem):
        self.eng, self.sem, self.base, self.n = eng, sem, 0, 0

    def did(self, ins):
        ins.then_inc(self.sem, 1)
        self.n += 1

    def wait(self):
        self.eng.wait_ge(self.sem, self.base + self.n)

    def turns(self, body, first, last, end, per_turn):
        for u in range(first):
            body(u)
        before, self.n = self.base + self.n, 0
        with self.eng.Fori(first, last) as u:
            self.base = (u - first) * per_turn + before
            body(u)
            assert self.n == per_turn, f"a turn of the loop has {self.n} signals"
        self.base, self.n = before + (last - first) * per_turn, 0
        for u in range(last, end):
            body(u)


def spread(ap, n):
    return ap.unsqueeze(2).to_broadcast([ap.shape[0], ap.shape[1], n])


def r32(ap):
    return ap.bitcast(F32)


def add_bias(bank, sb, tensor, n):
    rows = slice(GROUP * n, GROUP * n + 2)
    tensor.matmul(bank[:], sb["ones_r"][rows], sb["biases"][rows], start=True, stop=False)


def power_scale(v, st, largest, scale, inverse):
    st.did(v.tensor_scalar(largest, largest, SMALLEST, None, ALU.max)); st.wait()
    st.did(v.tensor_scalar(largest.bitcast(I32), largest.bitcast(I32), EXPONENT, None, ALU.bitwise_and)); st.wait()
    st.did(v.reciprocal(scale, largest))
    st.did(v.tensor_scalar(inverse, largest, 2.0 ** -14, None, ALU.mult)); st.wait()
    st.did(v.tensor_scalar(scale, scale, 2.0 ** 14, None, ALU.mult)); st.wait()


def prepare(nc, dram, sb, banks):
    with ExitStack() as own:
        def t(name, shape, dt):
            return own.enter_context(nc.sbuf_tensor(name, shape, dt))

        def sem(name):
            return own.enter_context(nc.semaphore(name))

        raw = sb["wi_hi"][:].rearrange("p e k n -> p (e k n)").bitcast(F32).rearrange(
            "p (i k n) -> p i k n", k=KD, n=D)
        wq_raw, wk_raw, wv_raw = raw[:, 0], raw[:, 1], raw[:, 2]
        bias, bv_all = raw[0:3 * GROUP, 3, 0], raw[:, 3, 1]
        side = t("side", [P, KD, SIDE], F32)
        zeros = t("zeros", [P, EXPERTS * REGION // P], I32)
        mx, mxa, scale, inv = (t(n, [P, 4], F32) for n in ("p_mx", "p_mxa", "p_scale", "p_inv"))
        side_max = t("side_max", [P, 2, KD], F32)
        rowno, rowf = t("rowno", [P, 2], I32), t("rowf", [P, 3], F32)
        second = t("second", [P, BLOCKS, 2], F32)
        onesf = t("onesf", [P, P], F32)

        wg_in, bias_in = sem("wg_in"), sem("bias_in")
        raw_in = [sem(f"raw_in{i}") for i in range(3)]
        consts = sem("consts")
        mx_ready, mxa_ready, scale_ready = sem("mx_ready"), sem("mxa_ready"), sem("scale_ready")
        high_done, dve_step, rows_ready = sem("high_done"), sem("prep_dve_step"), sem("rows_ready")
        stored = sem("prep_stored")

        ZEROED = 7
        with nc.Block() as block:
            @block.sync
            def _(sp):
                for n in range(3):
                    sp.dma_start(raw[GROUP * n:GROUP * n + GROUP, 3, 0], dram["biases"][n:n + 1, :].to_broadcast([GROUP, D])
                                 ).then_inc(bias_in, 16)
                sp.dma_start(bv_all, dram["biases"][3:4, :].to_broadcast([P, D])).then_inc(bias_in, 16)
                for n, (name, to) in enumerate((("wq", wq_raw), ("wk", wk_raw), ("wv", wv_raw))):
                    for i in range(2):
                        half = slice(KD // 2 * i, KD // 2 * (i + 1))
                        sp.dma_start(to[:, half], dram[name].rearrange("(k p) n -> p k n", p=P)[:, half]
                                     ).then_inc(raw_in[n], 16)
                sp.dma_start(side[:, :, DH:], dram["w_gate"].rearrange("(k p) e -> p k e", p=P)).then_inc(wg_in, 16)
                sp.wait_ge(consts, ZEROED)
                sp.dma_start(dram["lists"].rearrange("(p n) o -> p (n o)", p=P), zeros[:]).then_inc(stored, 16)
                sp.wait_ge(stored, 16)

            @block.gpsimd
            def _(pool):
                g = nc.gpsimd
                g.memset(sb["ident"][:], 0.0).then_inc(consts, 1)
                g.memset(sb["ident_bf"][:], 0.0).then_inc(consts, 1)
                g.memset(sb["below"][:], 1.0).then_inc(consts, 1)
                g.memset(sb["ones_bf"][:], 1.0).then_inc(consts, 1)
                g.memset(sb["mask"][:], 0.0).then_inc(consts, 1)
                g.memset(onesf[:], 1.0).then_inc(consts, 1)
                g.memset(zeros[:], 0).then_inc(consts, 1)
                g.iota(rowno[:], pattern=[[0, 2]], base=0, channel_multiplier=1).then_inc(rows_ready, 1)
                g.iota(second[:], pattern=[[0, BLOCKS], [HEADS, 2]], base=0, channel_multiplier=0,
                       allow_small_or_imprecise_dtypes=True).then_inc(rows_ready, 1)
                pool.wait_ge(consts, ZEROED)
                for m in (sb["ident"], sb["ident_bf"]):
                    g.affine_select(out=m[:], in_=m[:], compare_op=ALU.not_equal, fill=1.0, base=0,
                                    pattern=[[-1, P]], channel_multiplier=1).then_inc(consts, 1)
                g.affine_select(out=sb["below"][:], in_=sb["below"][:], compare_op=ALU.is_gt, fill=0.0,
                                base=0, pattern=[[1, P]], channel_multiplier=-1).then_inc(consts, 1)
                g.iota(sb["token"][:], pattern=[[P, TILES]], base=0, channel_multiplier=1)
                g.iota(sb["iota_e"][:], pattern=[[0, ROUTE_TILES], [1, EXPERTS]], base=-EXPERTS,
                       channel_multiplier=0, allow_small_or_imprecise_dtypes=True)
                g.iota(sb["count"][:], pattern=[[REGION, EXPERTS]], base=0, channel_multiplier=0,
                       allow_small_or_imprecise_dtypes=True)
                g.iota(sb["region"][:], pattern=[[REGION, EXPERTS]], base=0, channel_multiplier=0,
                       allow_small_or_imprecise_dtypes=True)
                n = ZEROED + 3
                for b in range(GROUPS):
                    part = sb["mask"][GROUP * b:GROUP * b + GROUP]
                    pool.wait_ge(consts, n)
                    g.affine_select(out=part, in_=part, compare_op=ALU.is_ge, fill=MASKED, base=0,
                                    pattern=[[0, BLOCKS], [-1, 2 * HEADS]], channel_multiplier=1).then_inc(consts, 1)
                    pool.wait_ge(consts, n + 1)
                    first = part[:, :, 0:HEADS]
                    g.affine_select(out=first, in_=first, compare_op=ALU.is_ge, fill=MASKED, base=HEADS - 1,
                                    pattern=[[0, BLOCKS], [0, HEADS]], channel_multiplier=-1).then_inc(consts, 1)
                    n += 2
                pool.wait_ge(consts, n)
                for n, cols in enumerate((slice(0, 1), slice(1, 2), slice(2, 4))):
                    after(pool, mxa_ready, n)
                    pool.wait_ge(mx_ready, n + 1)
                    g.partition_all_reduce(mxa[:, cols], mx[:, cols], P, REDUCE_MAX).then_inc(mxa_ready, 1)

            @block.scalar
            def _(act):
                for n, (name, item) in enumerate((("wq", wq_raw), ("wk", wk_raw))):
                    act.wait_ge(scale_ready, n + 1)
                    nc.scalar.activation(sb[name + "_hi"][:], item, ACT.Identity, scale=scale[:, n:n + 1]
                                         ).then_inc(high_done, 1)

            @block.vector
            def _(dve):
                v = nc.vector
                st = Steps(dve, dve_step)
                dve.wait_ge(consts, ZEROED)
                st.did(v.tensor_copy(sb["ones_r"][:], onesf[:]))
                dve.wait_ge(rows_ready, 2)
                st.did(v.tensor_scalar(rowno[:, 0:1], rowno[:, 0:1], GROUP - 1, None, ALU.bitwise_and))
                st.did(v.tensor_scalar(rowno[:, 1:2], rowno[:, 1:2], HEADS, None, ALU.bitwise_and)); st.wait()
                st.did(v.tensor_scalar(rowf[:, 0:1], rowno[:, 0:1], 0.0, None, ALU.is_equal))
                st.did(v.tensor_scalar(rowf[:, 1:2], rowno[:, 0:1], 1.0, None, ALU.is_equal))
                st.did(v.tensor_copy(rowf[:, 2:3], rowno[:, 1:2])); st.wait()
                st.did(v.tensor_scalar(sb["same_token"][:], second[:], rowf[:, 2:3], None, ALU.is_equal))

                dve.wait_ge(bias_in, 64)
                rows = slice(0, 3 * GROUP)
                st.did(v.tensor_reduce(sb["bv"][:], bv_all.rearrange("p (h d) -> p d h", d=DH), AX, ALU.add))
                st.did(v.tensor_copy(sb["biases"][rows], bias)); st.wait()
                st.did(v.tensor_tensor(bias, bias, r32(sb["biases"][rows]), ALU.subtract)); st.wait()
                st.did(v.tensor_scalar(bias, bias, rowf[rows, 1:2], None, ALU.mult)); st.wait()
                st.did(v.scalar_tensor_tensor(out=sb["biases"][rows], in0=r32(sb["biases"][rows]),
                                              scalar=rowf[rows, 0:1], in1=bias, op0=ALU.mult, op1=ALU.add)); st.wait()

                def largest(col, numbers):
                    return v.tensor_reduce(mx[:, col:col + 1], numbers, AX, ALU.max, apply_absolute_value=True)

                def scales(n, cols):
                    dve.wait_ge(mxa_ready, n + 1)
                    power_scale(v, st, mxa[:, cols], scale[:, cols], inv[:, cols])
                    dve.sem_inc(scale_ready, 1)

                def low(n, name, item):
                    dve.wait_ge(high_done, n + 1)
                    v.scalar_tensor_tensor(out=sb[name + "_lo"][:], in0=item, scalar=scale[:, n:n + 1],
                                           in1=sb[name + "_hi"][:], op0=ALU.mult, op1=ALU.subtract)

                for n, item in enumerate((wq_raw, wk_raw)):
                    dve.wait_ge(raw_in[n], 32)
                    largest(n, item.rearrange("p k n -> p (k n)")).then_inc(mx_ready, 1)
                    if n == 0:
                        scales(0, slice(0, 1))
                dve.wait_ge(raw_in[2], 32)
                for k in range(KD):
                    st.did(v.tensor_reduce(side[:, k, 0:DH], wv_raw[:, k].rearrange("p (h d) -> p d h", d=DH),
                                           AX, ALU.add))
                dve.wait_ge(wg_in, 16)
                st.wait()
                for k in range(KD):
                    st.did(v.tensor_reduce(side_max[:, 0, k:k + 1], side[:, k, 0:DH], AX, ALU.max,
                                           apply_absolute_value=True))
                    st.did(v.tensor_reduce(side_max[:, 1, k:k + 1], side[:, k, DH:], AX, ALU.max,
                                           apply_absolute_value=True))
                st.wait()
                v.tensor_reduce(mx[:, 2:4], side_max[:], AX, ALU.max).then_inc(mx_ready, 1)
                scales(1, slice(1, 2))
                low(0, "wq", wq_raw)
                scales(2, slice(2, 4))
                st.did(v.tensor_copy(sb["side_inv"][:], inv[:, 2:4]))
                for cols, n in ((slice(0, DH), 2), (slice(DH, SIDE), 3)):
                    st.did(v.tensor_scalar(sb["side_hi"][:, :, cols], side[:, :, cols], scale[:, n:n + 1], None, ALU.mult))
                st.wait()
                for cols, n in ((slice(0, DH), 2), (slice(DH, SIDE), 3)):
                    st.did(v.scalar_tensor_tensor(out=sb["side_lo"][:, :, cols], in0=side[:, :, cols],
                                                  scalar=scale[:, n:n + 1], in1=sb["side_hi"][:, :, cols],
                                                  op0=ALU.mult, op1=ALU.subtract))
                st.did(v.tensor_tensor(sb["qk_inv"][:], inv[:, 0:1], inv[:, 1:2], ALU.mult))
                low(1, "wk", wk_raw)
                for i in range(2):
                    rows = slice(GROUP * i, GROUP * i + GROUP)
                    st.did(v.tensor_scalar(sb["biases"][rows], r32(sb["biases"][rows]), scale[rows, i:i + 1], None,
                                           ALU.mult))


def attend_and_route(nc, dram, sb, banks):
    with ExitStack() as own:
        def t(name, shape, dt):
            return own.enter_context(nc.sbuf_tensor(name, shape, dt))

        def sem(name):
            return own.enter_context(nc.semaphore(name))

        def two(name, shape, dt):
            return [t(f"{name}{i}", shape, dt) for i in range(2)]

        xs = [t(f"xs{i}", [P, D], F32) for i in range(XBUFS)]
        xT_hi, xT_lo = two("xT_hi", [P, KD, P], F16), two("xT_lo", [P, KD, P], F16)
        q_turned, k_turned = two("q_turned", [P, D], F32), t("k_turned", [P, D], F32)
        weight = t("weight", [P, BLOCKS, GROUP], F32)
        k_diag = two("k_diag", [P, BLOCKS, GROUPS, GROUP], F32)
        top = t("top", [P, BLOCKS], F32)
        total, scale = t("total", [P, ROUTE_TILES, BLOCKS], F32), t("scale", [P, ROUTE_TILES, BLOCKS], F32)
        halves = weight[:].rearrange("p b c -> p (b c)").rearrange("p (o i n) -> p o i n", o=2, i=ROUTE_TILES)
        sums = halves[:, 0].rearrange("p i (b t) -> p i b t", t=2)
        sumsT = halves[:, 1].rearrange("p i (t h) -> p i t h", t=2)
        stats, mv = two("stats", [P, 6], F32), two("mv", [P, 2], F32)
        rstd = two("rstd", [P, 1], F32)
        minus_half = t("minus_half", [P, 1], F32)
        wide = [P, ROUTE_TILES, EXPERTS]
        logits, one1, one2, tmp, rank = (t(n, wide, F32) for n in ("logits", "one1", "one2", "tmp", "rank"))
        chosen = t("chosen", wide, BF16)
        m1, m2, i1, i2 = (t(n, [P, ROUTE_TILES], F32) for n in ("m1", "m2", "i1", "i2"))
        place, number = t("place", [P, 2, ROUTE_TILES], I32), t("number", [P, ROUTE_TILES], I32)

        raw = t("raw", [P, KD, 2 * FF], F32)
        wo_raw = raw[:, 0:KF]
        mx, mxa, wi_scale, inv = (t(n, [P, 1], F32) for n in ("e_mx", "e_mxa", "wi_scale", "e_inv"))

        wi_in, wo_in, mx_ready, mxa_ready = sem("wi_in"), sem("wo_in"), sem("e_mx_ready"), sem("e_mxa_ready")
        wi_scale_ready, wi_hi_ready, wi_lo_ready = sem("wi_scale_ready"), sem("wi_hi_ready"), sem("wi_lo_ready")
        wo_hi_ready, wo_lo_ready = sem("wo_hi_ready"), sem("wo_lo_ready")
        experts_of, row_of, inv_of = sb["experts_of"], sb["row_of"], sb["inv_of"]
        need_i, need = t("need_i", [P, EXPERTS], I32), t("need", [P, EXPERTS], F32)
        ones8, end = t("ones8", [P, EXPERTS], F32), t("end", [P, EXPERTS], F32)
        start, shift = t("start", [P, EXPERTS], F32), t("shift", [P, EXPERTS], F32)
        step_to, expert_no = t("step_to", [P, EXPERTS], F32), t("expert_no", [P, EXPERTS], F32)
        spare = [buf[:].rearrange("p b g c -> p (b g c)") for buf in k_diag]
        n = SLOT_TILES
        pick, mine = (buf[:, 0:n * EXPERTS].rearrange("p (t e) -> p t e", e=EXPERTS) for buf in spare)
        of_tile, begin, five = (spare[0][:, n * (EXPERTS + i):n * (EXPERTS + i + 1)] for i in range(3))
        ones, tile_no = (spare[1][:, n * (EXPERTS + i):n * (EXPERTS + i + 1)] for i in range(2))
        five = five[:, 0:n // 4 + 1]
        x_in = [sem(f"x_in{i}") for i in range(XBUFS)]
        xn_out = [sem(f"xn_out{i}") for i in range(XBUFS)]
        var_ready, rstd_ready, xn_ready = sem("var_ready"), sem("rstd_ready"), sem("xn_ready")
        turned, hi_ready, lo_ready = sem("turned"), sem("hi_ready"), sem("lo_ready")
        q_done, k_done, side_done = sem("q_done"), sem("k_done"), sem("side_done")
        qt_ready, kt_ready, k_diag_ready = sem("qt_ready"), sem("kt_ready"), sem("k_diag_ready")
        side_copied = sem("side_copied")
        scores_done, top_ready, centred, exp_ready = (sem(n) for n in ("scores_done", "top_ready", "centred", "exp_ready"))
        chosen_ready, ranks_done = sem("chosen_ready"), sem("ranks_done")
        place_ready, number_ready, scattered = sem("place_ready"), sem("number_ready"), sem("scattered")
        expert_no_ready = sem("expert_no_ready")
        pool_gate, pool_consts, dve_gate = sem("pool_gate"), sem("pool_consts"), sem("dve_gate")
        dve_step = sem("route_dve_step")

        T = ROUTE_TILES
        NB = TILES // T
        BANK_XS = banks[0:2]
        BANK_Q, BANK_K, BANK_S, BANK_SIDE, BANK_RANK = banks[2:7]
        ps_rank = BANK_RANK[:, 0:T * EXPERTS]
        ps_total = BANK_RANK[:, 256:256 + EXPERTS]
        ps_side = BANK_SIDE[:, 0:T * SIDE].rearrange("p (t c) -> p t c", c=SIDE)

        def of_expert(ap, e):
            return ap[:, bass.ds(e, 1)].rearrange("p o k n -> p (o k) n")

        def lagged(u, s, lag):
            return T * u + s - lag, (s - lag) % XBUFS, T // XBUFS * u + (s - lag) // XBUFS

        with nc.Block() as block:
            @block.sync
            def _(sp):
                def body(u):
                    for s in range(T):
                        i, b, before = lagged(u, s, 0)
                        if in_range(i, TILES):
                            after(sp, turned, i - XBUFS + 1)
                            after(sp, xn_out[b], 16 * before)
                            sp.dma_start(xs[b][:], dram["x_rows"][bass.ds(i * P, P), :]).then_inc(x_in[b], 16)
                        i, b, _ = lagged(u, s, 1)
                        if in_range(i, TILES):
                            sp.wait_ge(xn_ready, i + 1)
                            sp.dma_start(dram["xn_rows"][bass.ds(i * P, P), :], xs[b][:]).then_inc(xn_out[b], 16)

                turns(sp, body, 1, NB, NB + 1)
                for b in range(XBUFS):
                    sp.wait_ge(xn_out[b], 16 * TILES // XBUFS)

            @block.gpsimd
            def _(pool):
                g = nc.gpsimd
                g.memset(minus_half[:], -0.5).then_inc(pool_consts, 1)
                g.memset(ones8[:], 1.0)
                g.iota(expert_no[:], pattern=[[1, EXPERTS]], base=0, channel_multiplier=0,
                       allow_small_or_imprecise_dtypes=True).then_inc(expert_no_ready, 1)
                for buf in k_diag:
                    g.memset(buf[:], 0.0).then_inc(pool_consts, 1)
                pool.wait_ge(pool_consts, 1)

                def scatter(u, part):
                    if part == 0:
                        after(pool, scattered, 16 * 2 * T * u)
                        pool.sem_inc(pool_gate, 1)
                        g.tensor_copy(number[:], sb["token"][:, bass.ds(T * u, T)]).then_inc(number_ready, 1)
                        pool.wait_ge(number_ready, u + 1)
                        pool.wait_ge(place_ready, u + 1)
                        pool.sem_inc(pool_gate, 1)
                    for j in range(part * 3, min(T, part * 3 + 3)):
                        for k in range(2):
                            pool.indirect_dma_start(dram["lists"], IndirectOffsetOnAxis(place[:, k, j:j + 1], 0),
                                                    number[:, j:j + 1], None).then_inc(scattered, 16)

                def body(u):
                    for s in range(T):
                        i = T * u + s
                        if in_range(i, TILES):
                            pool.wait_ge(var_ready, i + 1)
                            g.tensor_tensor(rstd[s % 2][:], rstd[s % 2][:], minus_half[:], ALU.pow).then_inc(rstd_ready, 1)
                        if s == 7 and in_range(u, EXPERTS):
                            pool.wait_ge(mx_ready, u + 1)
                            pool.sem_inc(pool_gate, 1)
                            g.partition_all_reduce(mxa[:], mx[:], P, REDUCE_MAX).then_inc(mxa_ready, 1)
                        if s == 4 and in_range(u - 1, EXPERTS):
                            pool.wait_ge(wo_hi_ready, u)
                            g.tensor_tensor(of_expert(sb["wo_lo"], u - 1), wo_raw,
                                            of_expert(r32(sb["wo_hi"][:]), u - 1), ALU.subtract).then_inc(wo_lo_ready, 1)
                        if s >= 5 and in_range(u - 1, NB):
                            scatter(u - 1, s - 5)

                turns(pool, body, 2, NB, NB + 1)
                pool.wait_ge(scattered, 16 * 2 * T * NB)

            @block.scalar
            def _(act):
                a = nc.scalar
                act.wait_ge(pool_consts, 3)

                def body(u):
                    for s in range(T):
                        i, par = T * u + s - 1, (s - 1) % 2
                        if in_range(i, TILES):
                            act.wait_ge(turned, i + 1)
                            after(act, side_done, i - 1)
                            a.activation(xT_hi[par][:].rearrange("p k t -> p (k t)"), BANK_XS[par][:], ACT.Copy
                                         ).then_inc(hi_ready, 1)
                        i = T * u + s - 4
                        if in_range(i, TILES):
                            act.wait_ge(centred, i + 1)
                            a.activation(weight[:], weight[:], ACT.Exp, scale=SCORE_SCALE).then_inc(exp_ready, 1)
                        i = T * u + s - 2
                        if in_range(i, TILES):
                            act.wait_ge(kt_ready, i + 1)
                            after(act, scores_done, i - 1)
                            for group in range(GROUPS):
                                part = slice(GROUP * group, GROUP * group + GROUP)
                                last = a.activation(k_diag[s % 2][part, :, group, :],
                                                    k_turned[part, :].rearrange("p (b c) -> p b c", c=GROUP), ACT.Copy,
                                                    scale=sb["qk_inv"][part])
                            last.then_inc(k_diag_ready, 1)
                        if s == 7 and in_range(u, EXPERTS):
                            act.wait_ge(wi_scale_ready, u + 1)
                            a.activation(of_expert(sb["wi_hi"], u), raw[:], ACT.Identity, scale=wi_scale[:]
                                         ).then_inc(wi_hi_ready, 1)
                        if s == 1 and in_range(u - 1, EXPERTS):
                            act.wait_ge(wi_lo_ready, u)
                            act.dma_start(wo_raw, dram["wo"][bass.ds(u - 1, 1)].rearrange("o (k p) n -> p (o k) n", p=P)
                                          ).then_inc(wo_in, 16)
                        if s == 5 and in_range(u, EXPERTS):
                            after(act, wo_lo_ready, u)
                            for k in range(2):
                                act.dma_start(raw[:, :, FF * k:FF * k + FF],
                                              dram[f"wi_{k}"][bass.ds(u, 1)].rearrange("o (k p) n -> p (o k) n", p=P)
                                              ).then_inc(wi_in, 16)
                        if s == 3 and in_range(u - 1, EXPERTS):
                            act.wait_ge(wo_in, 16 * u)
                            a.activation(of_expert(sb["wo_hi"], u - 1), wo_raw, ACT.Copy).then_inc(wo_hi_ready, 1)

                turns(act, body, 1, NB, NB + 1)

            @block.vector
            def _(dve):
                v = nc.vector
                st = Steps(dve, dve_step)

                def choose_first(u):
                    dve.wait_ge(side_copied, u + 1)
                    st.did(v.tensor_reduce(m1[:], logits[:], AX, ALU.max)); st.wait()
                    st.did(v.tensor_tensor(tmp[:], logits[:], spread(m1[:], EXPERTS), ALU.is_equal)); st.wait()
                    st.did(v.scalar_tensor_tensor(out=tmp[:], in0=tmp[:], scalar=-float(EXPERTS), in1=sb["iota_e"][:],
                                                  op0=ALU.mult, op1=ALU.add)); st.wait()
                    st.did(v.tensor_reduce(i1[:], tmp[:], AX, ALU.min)); st.wait()
                    st.did(v.tensor_scalar(i1[:], i1[:], float(EXPERTS), None, ALU.add)); st.wait()
                    st.did(v.tensor_tensor(one1[:], sb["iota_e"][:], spread(i1[:], EXPERTS), ALU.is_equal)); st.wait()
                    st.did(v.scalar_tensor_tensor(out=logits[:], in0=one1[:], scalar=-3e38, in1=logits[:],
                                                  op0=ALU.mult, op1=ALU.add))

                def choose_second(u):
                    st.wait()
                    st.did(v.tensor_reduce(m2[:], logits[:], AX, ALU.max)); st.wait()
                    st.did(v.tensor_tensor(tmp[:], logits[:], spread(m2[:], EXPERTS), ALU.is_equal)); st.wait()
                    st.did(v.scalar_tensor_tensor(out=tmp[:], in0=tmp[:], scalar=-float(EXPERTS), in1=sb["iota_e"][:],
                                                  op0=ALU.mult, op1=ALU.add)); st.wait()
                    st.did(v.tensor_reduce(i2[:], tmp[:], AX, ALU.min)); st.wait()
                    st.did(v.tensor_scalar(i2[:], i2[:], float(EXPERTS), None, ALU.add)); st.wait()
                    st.did(v.tensor_tensor(one2[:], sb["iota_e"][:], spread(i2[:], EXPERTS), ALU.is_equal)); st.wait()
                    st.did(v.tensor_tensor(sb["gap"][:, bass.ds(T * u, T)], m2[:], m1[:], ALU.subtract))
                    v.tensor_tensor(chosen[:], one1[:], one2[:], ALU.add).then_inc(chosen_ready, 1)

                def copy_side(u):
                    dve.wait_ge(side_done, T * (u + 1))
                    v.scalar_tensor_tensor(out=sb["value_sum"][:, bass.ds(T * u, T), :], in0=ps_side[:, :, 0:DH],
                                           scalar=sb["side_inv"][:, 0:1],
                                           in1=sb["bv"][:].unsqueeze(1).to_broadcast([P, T, DH]),
                                           op0=ALU.mult, op1=ALU.add)
                    v.tensor_scalar(logits[:], ps_side[:, :, DH:], sb["side_inv"][:, 1:2], None, ALU.mult
                                    ).then_inc(side_copied, 1)

                def sum_weights(u):
                    st.wait()
                    st.did(v.reciprocal(scale[:], total[:])); st.wait()
                    st.did(v.tensor_tensor(total[:], total[:], scale[:], ALU.mult)); st.wait()
                    many = [P, T, BLOCKS, 2]
                    st.did(v.tensor_tensor(sums, total[:].unsqueeze(3).to_broadcast(many),
                                           sb["same_token"][:].unsqueeze(1).to_broadcast(many), ALU.mult)); st.wait()
                    st.did(v.transpose(sumsT.rearrange("p i t h -> p (i t h)"),
                                       sums.rearrange("p i b t -> p (i b t)"))); st.wait()
                    st.did(v.tensor_tensor(sb["weight_sum"][:, bass.ds(T * u, T), :],
                                           sumsT[:, :, 0, :], sumsT[:, :, 1, :], ALU.add))

                def place_tokens(u):
                    dve.wait_ge(ranks_done, u + 1)
                    st.did(v.tensor_tensor(rank[:], ps_rank.rearrange("p (t e) -> p t e", e=EXPERTS),
                                           sb["count"][:].unsqueeze(1).to_broadcast(wide), ALU.add)); st.wait()
                    st.did(v.tensor_tensor(sb["count"][:], sb["count"][:], ps_total, ALU.add))
                    after(dve, scattered, 16 * 2 * T * u)
                    for k, one in ((0, one1), (1, one2)):
                        st.did(v.tensor_tensor(tmp[:], one[:], rank[:], ALU.mult)); st.wait()
                        at = sb["pos"][:, k, bass.ds(T * u, T)]
                        st.did(v.tensor_reduce(i1[:], tmp[:], AX, ALU.add)); st.wait()
                        st.did(v.tensor_copy(at, i1[:]))
                        if k:
                            v.tensor_copy(place[:, k, :], i1[:]).then_inc(place_ready, 1)
                        else:
                            st.did(v.tensor_copy(place[:, k, :], i1[:])); st.wait()

                def body(u):
                    for s in range(T):
                        i, b, before = lagged(u, s, 0)
                        par = s % 2
                        if in_range(i, TILES):
                            dve.wait_ge(x_in[b], 16 * (before + 1))
                            st.did(v.bn_stats(stats[par][:], xs[b][:])); st.wait()
                            dve.sem_inc(dve_gate, 1)
                            st.did(v.bn_aggr(mv[par][:], stats[par][:])); st.wait()
                            v.tensor_scalar(rstd[par][:], mv[par][:, 1:2], EPS, None, ALU.add).then_inc(var_ready, 1)
                        j = T * u + s - 4
                        if in_range(j, TILES):
                            dve.wait_ge(scores_done, j + 1)
                            scores = BANK_S[:].rearrange("p (b c) -> p b c", c=GROUP)
                            v.tensor_reduce(top[:], scores, AX, ALU.max).then_inc(top_ready, 1)
                            dve.wait_ge(top_ready, j + 1)
                            v.tensor_tensor(weight[:], scores, spread(top[:], GROUP), ALU.subtract).then_inc(centred, 1)
                        if in_range(i, TILES):
                            dve.wait_ge(rstd_ready, i + 1)
                            v.tensor_scalar(xs[b][:], xs[b][:], mv[par][:, 0:1], rstd[par][:, 0:1],
                                            ALU.subtract, ALU.mult).then_inc(xn_ready, 1)
                        i, par = T * u + s - 1, (s - 1) % 2
                        if in_range(i, TILES):
                            dve.wait_ge(hi_ready, i + 1)
                            v.tensor_tensor(xT_lo[par][:].rearrange("p k t -> p (k t)"), BANK_XS[par][:],
                                            xT_hi[par][:].rearrange("p k t -> p (k t)"), ALU.subtract
                                            ).then_inc(lo_ready, 1)
                        if in_range(j, TILES):
                            dve.wait_ge(exp_ready, j + 1)
                            st.did(v.tensor_reduce(total[:, (s - 4) % T, :], weight[:], AX, ALU.add))
                        j = T * u + s - 2
                        if in_range(j, TILES):
                            for done, bank, used, count, turned_to, ready in (
                                    (k_done, BANK_K, k_diag_ready, j, k_turned[:], kt_ready),
                                    (q_done, BANK_Q, scores_done, j - 1, q_turned[s % 2][:], qt_ready)):
                                dve.wait_ge(done, j + 1)
                                after(dve, used, count)
                                v.transpose(turned_to.rearrange("p (t h) -> p h t", h=HEADS),
                                            bank[:].rearrange("p (h d) -> p h d", h=HEADS)).then_inc(ready, 1)
                        if s == 0 and in_range(u - 1, EXPERTS):
                            dve.wait_ge(wi_hi_ready, u)
                            v.scalar_tensor_tensor(out=of_expert(sb["wi_lo"], u - 1), in0=raw[:], scalar=wi_scale[:],
                                                   in1=of_expert(sb["wi_hi"], u - 1), op0=ALU.mult, op1=ALU.subtract
                                                   ).then_inc(wi_lo_ready, 1)
                        if s == 1 and in_range(u - 1, NB):
                            copy_side(u - 1)
                            choose_first(u - 1)
                        if s == 2 and in_range(u - 1, NB):
                            choose_second(u - 1)
                        if s == 3 and in_range(u - 1, NB):
                            sum_weights(u - 1)
                        if s == 4 and in_range(u - 1, NB):
                            place_tokens(u - 1)
                        if s == 6 and in_range(u, EXPERTS):
                            dve.wait_ge(wi_in, 32 * (u + 1))
                            v.tensor_reduce(mx[:], raw[:].rearrange("p k n -> p (k n)"), AX, ALU.max,
                                            apply_absolute_value=True).then_inc(mx_ready, 1)
                        if s == 7 and in_range(u, EXPERTS):
                            dve.wait_ge(mxa_ready, u + 1)
                            power_scale(v, st, mxa[:], wi_scale[:], inv[:])
                            v.tensor_copy(sb["wi_inv"][:, bass.ds(u, 1)], inv[:]).then_inc(wi_scale_ready, 1)

                st.turns(body, 2, NB, NB + 1, 3 * T + 5 + 5 + 14 + 9)

                dve.wait_ge(expert_no_ready, 1)
                dve.wait_ge(scores_done, TILES)
                st.did(v.memset(ones, 1.0)); st.wait()
                st.did(v.tensor_tensor_scan(tile_no, ones, ones, -1.0, ALU.mult, ALU.add)); st.wait()
                N = SLOT_TILES
                many_tiles = [P, N, EXPERTS]

                def per_tile(ap):
                    return ap.unsqueeze(1).to_broadcast(many_tiles)

                st.did(v.scalar_tensor_tensor(out=need_i[:], in0=sb["count"][:], scalar=float(P - 1),
                                              in1=sb["region"][:], op0=ALU.add, op1=ALU.subtract)); st.wait()
                st.did(v.tensor_scalar(need_i[:], need_i[:], P.bit_length() - 1, None, ALU.arith_shift_right)); st.wait()
                st.did(v.tensor_copy(need[:], need_i[:])); st.wait()
                st.did(v.tensor_tensor_scan(end[:], ones8[:], need[:], 0.0, ALU.mult, ALU.add)); st.wait()
                st.did(v.tensor_tensor(start[:], end[:], need[:], ALU.subtract)); st.wait()
                st.did(v.tensor_tensor(pick, spread(tile_no[:], EXPERTS), per_tile(end[:]), ALU.is_ge)); st.wait()
                st.did(v.tensor_reduce(of_tile[:], pick, AX, ALU.add)); st.wait()
                st.did(v.tensor_scalar(of_tile[:], of_tile[:], float(EXPERTS - 1), None, ALU.min)); st.wait()
                quads = of_tile[:].rearrange("p (u t) -> p u t", t=4)
                st.did(v.memset(five[:], 0.0)); st.wait()
                for digit, (to, tile) in enumerate(((1, 2), (1, 3), (0, 0), (0, 1), (0, 2))):
                    part = five[:, to:to + N // 4]
                    st.did(v.scalar_tensor_tensor(out=part, in0=quads[:, :, tile], scalar=float(EXPERTS ** digit),
                                                  in1=part, op0=ALU.mult, op1=ALU.add)); st.wait()
                st.did(v.tensor_copy(experts_of[:], five[:]))
                st.did(v.tensor_tensor(mine, per_tile(expert_no[:]), spread(of_tile[:], EXPERTS), ALU.is_equal)); st.wait()
                st.did(v.tensor_tensor(pick, mine, per_tile(start[:]), ALU.mult)); st.wait()
                st.did(v.tensor_reduce(begin[:], pick, AX, ALU.add)); st.wait()
                st.did(v.tensor_tensor(begin[:], tile_no[:], begin[:], ALU.subtract)); st.wait()
                st.did(v.tensor_scalar(begin[:], begin[:], float(REGION // P - 1), float(P), ALU.min, ALU.mult)); st.wait()
                st.did(v.scalar_tensor_tensor(out=row_of[:], in0=of_tile[:], scalar=float(REGION), in1=begin[:],
                                              op0=ALU.mult, op1=ALU.add))
                st.did(v.tensor_tensor(pick, mine, per_tile(sb["wi_inv"][:]), ALU.mult)); st.wait()
                st.did(v.tensor_reduce(inv_of[:], pick, AX, ALU.add)); st.wait()
                st.did(v.scalar_tensor_tensor(out=shift[:], in0=start[:], scalar=float(P), in1=sb["region"][:],
                                              op0=ALU.mult, op1=ALU.subtract)); st.wait()
                st.did(v.tensor_copy(step_to[:, 0:1], shift[:, 0:1]))
                st.did(v.tensor_tensor(step_to[:, 1:], shift[:, 1:], shift[:, 0:EXPERTS - 1], ALU.subtract)); st.wait()
                for k in range(2):
                    part = pick[:, 0:TILES, :]
                    many = [P, TILES, EXPERTS]
                    st.did(v.tensor_tensor(part, spread(sb["pos"][:, k, :], EXPERTS),
                                           sb["region"][:].unsqueeze(1).to_broadcast(many), ALU.is_ge)); st.wait()
                    st.did(v.tensor_tensor(part, part, step_to[:].unsqueeze(1).to_broadcast(many), ALU.mult)); st.wait()
                    st.did(v.tensor_reduce(begin[:, 0:TILES], part, AX, ALU.add)); st.wait()
                    st.did(v.tensor_tensor(sb["slot"][:, k, :], begin[:, 0:TILES], sb["pos"][:, k, :], ALU.add)); st.wait()

            @block.tensor
            def _(pe):
                m = nc.tensor

                def product(out, par, weights_hi, weights_lo, start):
                    for k in range(KD):
                        m.matmul(out, xT_hi[par][:, k, :], weights_hi[:, k, :], start=start and k == 0, stop=False)
                        m.matmul(out, xT_hi[par][:, k, :], weights_lo[:, k, :], start=False, stop=False)
                        last = m.matmul(out, xT_lo[par][:, k, :], weights_hi[:, k, :], start=False, stop=k == KD - 1)
                    return last

                def ranks(u):
                    pe.wait_ge(chosen_ready, u + 1)
                    ch = chosen[:].rearrange("p t e -> p (t e)")
                    n = T * EXPERTS
                    m.matmul(ps_rank, sb["below"][:], ch, start=True, stop=False)
                    for d in range(1, T):
                        m.matmul(ps_rank[:, EXPERTS * d:n], sb["ones_bf"][:], ch[:, 0:n - EXPERTS * d],
                                 start=False, stop=d == T - 1)
                    for d in range(T):
                        last = m.matmul(ps_total, sb["ones_bf"][:], ch[:, EXPERTS * d:EXPERTS * d + EXPERTS],
                                        start=d == 0, stop=d == T - 1)
                    last.then_inc(ranks_done, 1)

                def body(u):
                    for s in range(T):
                        i, b, _ = lagged(u, s, 1)
                        par = (s - 1) % 2
                        if in_range(i, TILES):
                            pe.wait_ge(xn_ready, i + 1)
                            after(pe, lo_ready, i - 1)
                            for k in range(KD):
                                last = m.transpose(BANK_XS[par][:, P * k:P * k + P], xs[b][:, P * k:P * k + P],
                                                   sb["ident"][:])
                            last.then_inc(turned, 1)
                        j = T * u + s - 4
                        if in_range(j, TILES):
                            pe.wait_ge(k_diag_ready, j + 1)
                            pe.wait_ge(qt_ready, j + 1)
                            after(pe, centred, j)
                            m.matmul(BANK_S[:], sb["ident_bf"][:], sb["mask"][:].rearrange("p b c -> p (b c)"),
                                     start=True, stop=False)
                            for b in range(BLOCKS):
                                c, strip = b // GROUPS, slice(GROUP * (b % GROUPS), GROUP * (b % GROUPS) + GROUP)
                                last = m.matmul(BANK_S[strip, P * c:P * c + P], q_turned[s % 2][:, GROUP * b:GROUP * b + GROUP],
                                                k_diag[s % 2][:, b].rearrange("p g c -> p (g c)"),
                                                start=False, stop=c == BLOCKS // GROUPS - 1)
                            last.then_inc(scores_done, 1)
                        j, par = T * u + s - 2, s % 2
                        if in_range(j, TILES):
                            pe.wait_ge(hi_ready, j + 1)
                            pe.wait_ge(lo_ready, j + 1)
                            for n, bank, w, done, copied in ((1, BANK_K, "wk", k_done, kt_ready),
                                                             (0, BANK_Q, "wq", q_done, qt_ready)):
                                after(pe, copied, j)
                                add_bias(bank, sb, m, n)
                                product(bank[:], par, sb[w + "_hi"], sb[w + "_lo"], False).then_inc(done, 1)
                            if s == 2:
                                after(pe, side_copied, u)
                            product(ps_side[:, (s - 2) % T], par, sb["side_hi"], sb["side_lo"], True).then_inc(side_done, 1)
                        if s == 3 and in_range(u - 1, NB):
                            ranks(u - 1)

                turns(pe, body, 1, NB, NB + 1)


def experts(nc, dram, sb, banks):
    with ExitStack() as own:
        def t(name, shape, dt):
            return own.enter_context(nc.sbuf_tensor(name, shape, dt))

        def sem(name):
            return own.enter_context(nc.semaphore(name))

        def two(name, shape, dt):
            return [t(f"{name}{i}", shape, dt) for i in range(2)]

        experts_of, row_of, inv_of = sb["experts_of"], sb["row_of"], sb["inv_of"]
        half_inv, half_inv2 = t("half_inv", [P, SLOT_TILES], F32), t("half_inv2", [P, SLOT_TILES], F32)

        rows = two("rows", [P, 1], I32)
        xg = two("xg", [P, D], F32)
        xT_hi, xT_lo = two("xgT_hi", [P, KD, P], F16), two("xgT_lo", [P, KD, P], F16)
        th, gated, inter = two("th", [P, FF], F32), two("gated", [P, FF], F32), two("inter", [P, FF], F32)
        iT_hi, iT_lo = two("iT_hi", [P, KF, P], F32R), two("iT_lo", [P, KF, P], F32R)
        out = two("e_out", [P, D], F32)

        wout_raw = t("wout_raw", [P, KD, D], F32)
        wout_in, wout_hi_ready = sem("wout_in"), sem("wout_hi_ready")
        tables_ready = sem("tables_ready")
        rows_in = [sem("rows_in0"), sem("rows_in1")]
        gathered = [sem("gathered0"), sem("gathered1")]
        stored = [sem("e_stored0"), sem("e_stored1")]
        turned, hi_ready, lo_ready = sem("e_turned"), sem("e_hi_ready"), sem("e_lo_ready")
        up_done, th_ready, inter_ready = sem("up_done"), sem("th_ready"), sem("inter_ready")
        iturned, ihi_ready, ilo_ready = sem("iturned"), sem("ihi_ready"), sem("ilo_ready")
        down_done, out_ready = sem("down_done"), sem("out_ready")
        sp_gate = sem("e_sp_gate")
        pool_gate, gated_ready, dve_step = sem("e_pool_gate"), sem("gated_ready"), sem("e_dve_step")

        N = SLOT_TILES
        FIRST, LAST, LAG = 3, N // 2, 6
        END = (N + LAG) // 2 + 1

        def body_of(step):
            def body(u):
                for s in range(2):
                    step(2 * u + s, u, s)
            return body

        with nc.Block() as block:
            @block.sync
            def _(sp):
                sp.dma_start(wout_raw[:], dram["wout"].rearrange("(k p) n -> p k n", p=P)).then_inc(wout_in, 16)

                def step(j, u, s):
                    if in_range(j, N):
                        after(sp, gathered[s], 16 * u)
                        sp.sem_inc(sp_gate, 1)
                        at = sp.value_load(row_of[0:1, bass.ds(j, 1)], min_val=0, max_val=EXPERTS * REGION - P)
                        sp.dma_start(rows[s][:], dram["lists"][bass.ds(at, P), :]).then_inc(rows_in[s], 16)
                    i = j - LAG
                    if in_range(i, N):
                        sp.wait_ge(out_ready, i + 1)
                        sp.dma_start(dram["expert_rows"][bass.ds(i * P, P), :], out[s][:]).then_inc(stored[s], 16)

                turns(sp, body_of(step), FIRST, LAST, END)
                for s in range(2):
                    sp.wait_ge(stored[s], 16 * N // 2)

            @block.gpsimd
            def _(pool):
                g = nc.gpsimd
                def step(j, u, s):
                    if in_range(j, N):
                        after(pool, turned, j - 1)
                        pool.wait_ge(rows_in[s], 16 * (u + 1))
                        pool.sem_inc(pool_gate, 1)
                        pool.indirect_dma_start(xg[s][:], None, dram["xn_rows"],
                                                IndirectOffsetOnAxis(rows[s][:, 0:1], 0)).then_inc(gathered[s], 16)

                turns(pool, body_of(step), FIRST, LAST, LAST)

            @block.scalar
            def _(act):
                a = nc.scalar
                act.wait_ge(wout_in, 16)
                a.activation(sb["wout_hi"][:], wout_raw[:], ACT.Copy).then_inc(wout_hi_ready, 1)
                act.wait_ge(tables_ready, 1)

                def step(j, u, s):
                    if in_range(j, N):
                        act.wait_ge(turned, j + 1)
                        after(act, up_done, j - 1)
                        a.activation(xT_hi[s][:].rearrange("p k t -> p (k t)"), banks[s][:], ACT.Copy
                                     ).then_inc(hi_ready, 1)
                    i = j - 2
                    if in_range(i, N):
                        act.wait_ge(iturned, i + 1)
                        after(act, down_done, i - 1)
                        a.activation(iT_hi[s][:].rearrange("p k t -> p (k t)"), banks[4 + s][:, 0:FF], ACT.Copy
                                     ).then_inc(ihi_ready, 1)
                    i, o = j - 3, 1 - s
                    if in_range(i, N):
                        act.wait_ge(down_done, i + 1)
                        after(act, stored[o], 16 * (u - 2 + s))
                        a.activation(out[o][:], banks[6 + o][:], ACT.Copy).then_inc(out_ready, 1)
                    i = j - 1
                    if in_range(i, N):
                        act.wait_ge(up_done, i + 1)
                        after(act, gated_ready, i - 1)
                        a.activation(th[o][:], banks[2 + o][:, 0:FF], ACT.Tanh,
                                     scale=half_inv[:, bass.ds(i, 1)]).then_inc(th_ready, 1)

                turns(act, body_of(step), FIRST, LAST, END)

            @block.vector
            def _(dve):
                v = nc.vector
                st = Steps(dve, dve_step)

                st.did(v.tensor_scalar(half_inv[:], inv_of[:], 0.5, None, ALU.mult)); st.wait()
                st.did(v.tensor_tensor(half_inv2[:], half_inv[:], inv_of[:], ALU.mult)); st.wait()
                dve.sem_inc(tables_ready, 1)

                def step(j, u, s):
                    if in_range(j, N):
                        dve.wait_ge(hi_ready, j + 1)
                        v.tensor_tensor(xT_lo[s][:].rearrange("p k t -> p (k t)"), banks[s][:],
                                        xT_hi[s][:].rearrange("p k t -> p (k t)"), ALU.subtract).then_inc(lo_ready, 1)
                    i = j - 2
                    if in_range(i, N):
                        dve.wait_ge(ihi_ready, i + 1)
                        v.tensor_tensor(iT_lo[s][:].rearrange("p k t -> p (k t)"), banks[4 + s][:, 0:FF],
                                        r32(iT_hi[s][:]).rearrange("p k t -> p (k t)"), ALU.subtract
                                        ).then_inc(ilo_ready, 1)
                    i, o = j - 1, 1 - s
                    if in_range(i, N):
                        dve.wait_ge(th_ready, i + 1)
                        v.scalar_tensor_tensor(out=gated[o][:], in0=th[o][:], scalar=1.0, in1=banks[2 + o][:, 0:FF],
                                               op0=ALU.add, op1=ALU.mult).then_inc(gated_ready, 1)
                        dve.wait_ge(gated_ready, i + 1)
                        after(dve, iturned, i - 1)
                        v.scalar_tensor_tensor(out=inter[o][:], in0=banks[2 + o][:, FF:2 * FF],
                                               scalar=half_inv2[:, bass.ds(i, 1)], in1=gated[o][:],
                                               op0=ALU.mult, op1=ALU.mult).then_inc(inter_ready, 1)

                turns(dve, body_of(step), FIRST, LAST, END)
                dve.wait_ge(wout_hi_ready, 1)
                v.tensor_tensor(sb["wout_lo"][:], wout_raw[:], r32(sb["wout_hi"][:]), ALU.subtract)

            @block.tensor
            def _(pe):
                m = nc.tensor

                def load_experts(u):
                    five = pe.value_load(experts_of[0:1, bass.ds(u, 1)], min_val=0, max_val=EXPERTS ** 5 - 1)
                    return [five // EXPERTS ** i % EXPERTS for i in range(5)]

                def weights(name, e, k):
                    return sb[name][:, bass.ds(e, 1), k, :].rearrange("p o n -> p (o n)")

                def up(i, o, e, chunks):
                    for k in chunks:
                        m.matmul(banks[2 + o][:], xT_hi[o][:, k, :], weights("wi_hi", e, k), start=k == 0, stop=False)
                        m.matmul(banks[2 + o][:], xT_hi[o][:, k, :], weights("wi_lo", e, k), start=False, stop=False)
                        last = m.matmul(banks[2 + o][:], xT_lo[o][:, k, :], weights("wi_hi", e, k), start=False,
                                        stop=k == KD - 1)
                    return last

                def body(u):
                    e = load_experts(u) if in_range(u, N // 4 + 1) else (None,) * 5
                    for s in range(4):
                        step(4 * u + s, 2 * u + s // 2, s % 2, e[s + 1], e[s])

                def step(j, u, s, e_up, e_down):
                    o = 1 - s
                    if in_range(j, N):
                        pe.wait_ge(gathered[s], 16 * (u + 1))
                        after(pe, lo_ready, j - 1)
                        for k in range(KD):
                            last = m.transpose(banks[s][:, P * k:P * k + P], xg[s][:, P * k:P * k + P], sb["ident"][:])
                        last.then_inc(turned, 1)
                    i = j - 1
                    if in_range(i, N):
                        pe.wait_ge(hi_ready, i + 1)
                        pe.wait_ge(lo_ready, i + 1)
                        after(pe, inter_ready, i - 1)
                        up(i, o, e_up, range(1))
                    i = j - 2
                    if in_range(i, N):
                        pe.wait_ge(inter_ready, i + 1)
                        after(pe, ilo_ready, i - 1)
                        for k in range(KF):
                            last = m.transpose(banks[4 + s][:, P * k:P * k + P], inter[s][:, P * k:P * k + P],
                                               sb["ident"][:])
                        last.then_inc(iturned, 1)
                    i = j - 1
                    if in_range(i, N):
                        up(i, o, e_up, range(1, KD)).then_inc(up_done, 1)
                    i = j - 2
                    if in_range(i, N):
                        pe.wait_ge(ihi_ready, i + 1)
                        pe.wait_ge(ilo_ready, i + 1)
                        after(pe, out_ready, i - 1)
                        for k in range(KF):
                            m.matmul(banks[6 + s][:], iT_hi[s][:, k, :], weights("wo_hi", e_down, k), start=k == 0,
                                     stop=False)
                            m.matmul(banks[6 + s][:], iT_hi[s][:, k, :], weights("wo_lo", e_down, k), start=False,
                                     stop=False)
                            last = m.matmul(banks[6 + s][:], iT_lo[s][:, k, :], weights("wo_hi", e_down, k), start=False,
                                            stop=k == KF - 1)
                        last.then_inc(down_done, 1)

                turns(pe, body, 2, N // 4, (N + LAG) // 4 + 1)


def combine(nc, dram, sb, banks):
    with ExitStack() as own:
        def t(name, shape, dt):
            return own.enter_context(nc.sbuf_tensor(name, shape, dt))

        def sem(name):
            return own.enter_context(nc.semaphore(name))

        def four(name, shape, dt):
            return [t(f"{name}{i}", shape, dt) for i in range(4)]

        w1, w2, ew = (t(n, [P, TILES], F32) for n in ("w1", "w2", "ew"))
        heads = four("heads", [P, HEADS, DH], F32)
        hT_hi, hT_lo = four("hT_hi", [P, HC, P], F32R), four("hT_lo", [P, HC, P], F32R)
        idx, ya, yb = four("idx", [P, 2], I32), four("ya", [P, D], F32), four("yb", [P, D], F32)
        part, mixed, th, gate = (four(n, [P, D], F32) for n in ("part", "mixed", "g_th", "gate"))
        x_in, gated, final = four("xr", [P, D], F32), four("y_gated", [P, D], F32), four("final", [P, D], F32)

        turn_rows = t("turn_rows", [P, P], F32)
        weight_sum = t("weight_sum_ordered", [P, TILES, HEADS], F32)

        wts, order_ready, ordered, order_copied = sem("wts"), sem("order_ready"), sem("ordered"), sem("order_copied")
        x_got = [sem(f"x_got{i}") for i in range(4)]
        fetched = [sem(f"fetched{i}") for i in range(4)]
        stored = [sem(f"f_stored{i}") for i in range(4)]
        heads_ready, h_turned, hT_hi_ready, hT_lo_ready = (
            sem(n) for n in ("heads_ready", "h_turned", "hT_hi_ready", "hT_lo_ready"))
        idx_ready, pool_gate, dve_gate = sem("idx_ready"), sem("c_pool_gate"), sem("c_dve_gate")
        part_ready, mixed_ready, th_ready, gate_ready = (
            sem(n) for n in ("part_ready", "mixed_ready", "c_th_ready", "gate_ready"))
        y_done, gated_ready = sem("y_done"), sem("c_gated_ready")
        final_ready = [sem(f"final_ready{i}") for i in range(4)]
        BY_DVE = 3

        N = TILES
        FIRST, LAST, LAG = 3, N // 4 - 1, 8
        END = (N + LAG) // 4
        BANK_H, BANK_Y = banks[0:4], banks[4:8]

        def body_of(step):
            def body(u):
                for s in range(4):
                    step(lambda lag: (4 * u + s - lag, (s - lag) % 4, u + (s - lag) // 4))
            return body

        with nc.Block() as block:
            @block.sync
            def _(sp):
                def step(at):
                    j, b, before = at(3)
                    if in_range(j, N):
                        after(sp, final_ready[b], before)
                        sp.dma_start(x_in[b][:], dram["x_rows"][bass.ds(j * P, P), :]).then_inc(x_got[b], 16)
                    j, b, before = at(6)
                    if in_range(j, N):
                        sp.wait_ge(final_ready[b], before + 1)
                        sp.dma_start(dram["out"][bass.ds(j * P, P), :], final[b][:]).then_inc(stored[b], 16)

                turns(sp, body_of(step), FIRST, LAST, END)
                for b in range(4):
                    sp.wait_ge(stored[b], 16 * N // 4)

            @block.gpsimd
            def _(pool):
                g = nc.gpsimd
                to = turn_rows[:].rearrange("p (g c j t) -> p g c j t", g=GROUPS, c=GROUPS, t=2)
                frm = sb["ident"][:].rearrange("p (j c g t) -> p g c j t", g=GROUPS, c=GROUPS, t=2)
                for i in range(GROUPS):
                    g.tensor_copy(to[:, i], frm[:, i]).then_inc(order_ready, 1)

                def step(at):
                    j, b, before = at(0)
                    if in_range(j, N):
                        after(pool, fetched[b], 32 * before)
                        after(pool, mixed_ready, j - 3)
                        pool.wait_ge(idx_ready, j + 1)
                        pool.sem_inc(pool_gate, 1)
                        for k, to in ((0, ya[b]), (1, yb[b])):
                            pool.indirect_dma_start(to[:], None, dram["expert_rows"],
                                                    IndirectOffsetOnAxis(idx[b][:, k:k + 1], 0)
                                                    ).then_inc(fetched[b], 16)
                    j, b, before = at(5)
                    if in_range(j, N) and b != BY_DVE:
                        pool.wait_ge(gated_ready, j + 1)
                        pool.wait_ge(x_got[b], 16 * (before + 1))
                        after(pool, stored[b], 16 * before)
                        pool.sem_inc(pool_gate, 1)
                        g.tensor_tensor(final[b][:], gated[b][:], x_in[b][:], ALU.add).then_inc(final_ready[b], 1)

                turns(pool, body_of(step), FIRST, LAST, END)

            @block.scalar
            def _(act):
                a = nc.scalar
                a.activation(ew[:], sb["gap"][:], ACT.Exp).then_inc(wts, 1)
                act.wait_ge(wts, 4)

                def step(at):
                    j, b, _ = at(1)
                    if in_range(j, N):
                        act.wait_ge(h_turned, j + 1)
                        after(act, y_done, j - 3)
                        a.activation(hT_hi[b][:].rearrange("p c t -> p (c t)"), BANK_H[b][:], ACT.Copy
                                     ).then_inc(hT_hi_ready, 1)
                    j, b, before = at(2)
                    if in_range(j, N):
                        act.wait_ge(fetched[b], 32 * (before + 1))
                        after(act, mixed_ready, j - 3)
                        a.activation(part[b][:], ya[b][:], ACT.Copy, scale=w1[:, bass.ds(j, 1)]).then_inc(part_ready, 1)
                    j, b, _ = at(3)
                    if in_range(j, N):
                        act.wait_ge(mixed_ready, j + 1)
                        after(act, gate_ready, j - 3)
                        a.activation(th[b][:], mixed[b][:], ACT.Tanh, scale=0.5).then_inc(th_ready, 1)

                turns(act, body_of(step), FIRST, LAST, END)

            @block.vector
            def _(dve):
                v = nc.vector
                dve.wait_ge(wts, 1)
                v.tensor_scalar(w2[:], ew[:], 1.0, None, ALU.add).then_inc(wts, 1)
                dve.wait_ge(wts, 2)
                v.reciprocal(w1[:], w2[:]).then_inc(wts, 1)
                dve.wait_ge(wts, 3)
                v.tensor_tensor(w2[:], ew[:], w1[:], ALU.mult).then_inc(wts, 1)
                dve.wait_ge(wts, 4)
                dve.wait_ge(ordered, 1)
                for n in range(2):
                    half = slice(TILES // 2 * n, TILES // 2 * (n + 1))
                    v.tensor_copy(weight_sum[:, half, :].rearrange("p i h -> p (i h)"), BANK_Y[n][:]
                                  ).then_inc(order_copied, 1)
                dve.wait_ge(order_copied, 2)
                v.tensor_copy(idx[0][:], sb["slot"][:, :, 0]).then_inc(idx_ready, 1)

                def step(at):
                    j, b, before = at(-1)
                    if in_range(j, N):
                        after(dve, fetched[b], 32 * before)
                        v.tensor_copy(idx[b][:], sb["slot"][:, :, bass.ds(j, 1)].rearrange("p k o -> p (k o)")
                                      ).then_inc(idx_ready, 1)
                    j, b, _ = at(0)
                    if in_range(j, N):
                        after(dve, h_turned, j - 3)
                        v.tensor_tensor(heads[b][:], spread(weight_sum[:, bass.ds(j, 1), :].rearrange(
                                            "p o h -> p (o h)"), DH),
                                        sb["value_sum"][:, bass.ds(j, 1), :].to_broadcast([P, HEADS, DH]), ALU.mult
                                        ).then_inc(heads_ready, 1)
                    j, b, _ = at(2)
                    if in_range(j, N):
                        dve.wait_ge(part_ready, j + 1)
                        after(dve, gate_ready, j - 3)
                        v.scalar_tensor_tensor(out=mixed[b][:], in0=yb[b][:], scalar=w2[:, bass.ds(j, 1)],
                                               in1=part[b][:], op0=ALU.mult, op1=ALU.add).then_inc(mixed_ready, 1)
                    j, b, _ = at(1)
                    if in_range(j, N):
                        dve.wait_ge(hT_hi_ready, j + 1)
                        after(dve, y_done, j - 3)
                        v.tensor_tensor(hT_lo[b][:].rearrange("p c t -> p (c t)"), BANK_H[b][:],
                                        r32(hT_hi[b][:]).rearrange("p c t -> p (c t)"), ALU.subtract
                                        ).then_inc(hT_lo_ready, 1)
                    j, b, _ = at(3)
                    if in_range(j, N):
                        dve.wait_ge(th_ready, j + 1)
                        v.scalar_tensor_tensor(out=gate[b][:], in0=th[b][:], scalar=1.0, in1=mixed[b][:],
                                               op0=ALU.add, op1=ALU.mult).then_inc(gate_ready, 1)
                    j, b, before = at(5)
                    if in_range(j, N) and b == BY_DVE:
                        dve.wait_ge(gated_ready, j + 1)
                        dve.wait_ge(x_got[b], 16 * (before + 1))
                        after(dve, stored[b], 16 * before)
                        v.tensor_tensor(final[b][:], gated[b][:], x_in[b][:], ALU.add).then_inc(final_ready[b], 1)
                    j, b, before = at(4)
                    if in_range(j, N):
                        dve.wait_ge(y_done, j + 1)
                        after(dve, final_ready[b], before)
                        dve.wait_ge(gate_ready, j + 1)
                        v.scalar_tensor_tensor(out=gated[b][:], in0=BANK_Y[b][:], scalar=0.5, in1=gate[b][:],
                                               op0=ALU.mult, op1=ALU.mult).then_inc(gated_ready, 1)

                turns(dve, body_of(step), FIRST, LAST, END)

            @block.tensor
            def _(pe):
                m = nc.tensor
                pe.wait_ge(order_ready, GROUPS)
                for n in range(2):
                    half = slice(TILES // 2 * n, TILES // 2 * (n + 1))
                    last = m.matmul(BANK_Y[n][:], turn_rows[:], sb["weight_sum"][:, half, :].rearrange("p i h -> p (i h)"),
                                    start=True, stop=True)
                last.then_inc(ordered, 1)
                pe.wait_ge(order_copied, 2)

                def step(at):
                    j, b, _ = at(1)
                    if in_range(j, N):
                        pe.wait_ge(heads_ready, j + 1)
                        after(pe, hT_lo_ready, j - 3)
                        for c in range(HC):
                            last = m.transpose(BANK_H[b][:, P * c:P * c + P],
                                               heads[b][:].rearrange("p h d -> p (h d)")[:, P * c:P * c + P],
                                               sb["ident"][:])
                        last.then_inc(h_turned, 1)
                    j, b, _ = at(2)
                    if in_range(j, N):
                        pe.wait_ge(hT_hi_ready, j + 1)
                        pe.wait_ge(hT_lo_ready, j + 1)
                        after(pe, gated_ready, j - 3)
                        out, w_hi, w_lo = BANK_Y[b], sb["wout_hi"][:], sb["wout_lo"][:]
                        add_bias(out, sb, m, 2)
                        for c in range(HC):
                            m.matmul(out[:], hT_hi[b][:, c, :], w_hi[:, c, :], start=False, stop=False)
                            m.matmul(out[:], hT_hi[b][:, c, :], w_lo[:, c, :], start=False, stop=False)
                            last = m.matmul(out[:], hT_lo[b][:, c, :], w_hi[:, c, :], start=False, stop=c == HC - 1)
                        last.then_inc(y_done, 1)

                turns(pe, body_of(step), FIRST, LAST, END)


def build(nc, dram):
    ctx = ExitStack()
    with ctx:
        def t(name, shape, dt):
            return ctx.enter_context(nc.sbuf_tensor(name, shape, dt))

        sb = {
            "side_hi": t("side_hi", [P, KD, SIDE], F16), "side_lo": t("side_lo", [P, KD, SIDE], F16),
            "side_inv": t("side_inv", [P, 2], F32), "qk_inv": t("qk_inv", [P, 1], F32),
            "biases": t("biases", [P, D], F32R), "bv": t("bv_sum", [P, DH], F32),
            "same_token": t("same_token", [P, BLOCKS, 2], F32),
            "weight_sum": t("weight_sum", [P, TILES, HEADS], F32), "value_sum": t("value_sum", [P, TILES, DH], F32),
            "ones_r": t("ones_r", [P, P], F32R),
            "ident": t("ident", [P, P], F32), "ident_bf": t("ident_bf", [P, P], BF16),
            "below": t("below", [P, P], BF16), "ones_bf": t("ones_bf", [P, P], BF16),
            "mask": t("mask", [P, BLOCKS, 2 * HEADS], BF16),
            "token": t("token", [P, TILES], I32),
            "iota_e": t("iota_e", [P, ROUTE_TILES, EXPERTS], F32),
            "count": t("count", [P, EXPERTS], F32), "region": t("region", [P, EXPERTS], F32),
            "wi_inv": t("wi_inv", [P, EXPERTS], F32),
            "gap": t("gap", [P, TILES], F32), "pos": t("pos", [P, 2, TILES], F32),
            "experts_of": t("experts_of", [P, SLOT_TILES // 4 + 1], I32), "row_of": t("row_of", [P, SLOT_TILES], I32),
            "inv_of": t("inv_of", [P, SLOT_TILES], F32),
        }
        sb["slot"] = sb["pos"][:].bitcast(I32)
        psum = ctx.enter_context(nc.psum_tensor("psum", [P, 8, 512], F32))
        banks = [psum[:, i, :] for i in range(8)]
        dram = dict(dram)
        for name, shape, dt in (
            ("xn_rows", [TOKENS, D], F32),
            ("lists", [EXPERTS * REGION, 1], I32), ("expert_rows", [SLOT_TILES * P, D], F32),
        ):
            dram[name] = nc.dram_tensor(name + "_scratch", shape, dt).ap()
        with ExitStack() as weights:
            def w(name, shape, dt):
                return weights.enter_context(nc.sbuf_tensor(name, shape, dt))

            sb |= {
                "wi_hi": w("wi_hi", [P, EXPERTS, KD, 2 * FF], F16), "wi_lo": w("wi_lo", [P, EXPERTS, KD, 2 * FF], F16),
                "wo_hi": w("wo_hi", [P, EXPERTS, KF, D], F32R), "wo_lo": w("wo_lo", [P, EXPERTS, KF, D], F32R),
            }
            with ExitStack() as keys:
                for name in ("wq_hi", "wq_lo", "wk_hi", "wk_lo"):
                    sb[name] = keys.enter_context(nc.sbuf_tensor(name, [P, KD, D], F16, side="right"))
                prepare(nc, dram, sb, banks)
                attend_and_route(nc, dram, sb, banks)
            for name in ("wout_hi", "wout_lo"):
                sb[name] = ctx.enter_context(nc.sbuf_tensor(name, [P, HC, D], F32R, side="right"))
            experts(nc, dram, sb, banks)
        combine(nc, dram, sb, banks)


def kernel(**inputs):
    import concourse.bacc as bacc
    from concourse.bass_utils import run_bass_kernel_spmd

    a = {k: np.asarray(v) for k, v in inputs.items()}
    w = a["L0_attn_Wqkv"]
    b = a["L0_attn_bqkv"]
    arrays = {
        "x_rows": a["L0_attn_x"].reshape(TOKENS, D),
        "wq": w[:, :, 0:DH].reshape(D, HEADS * DH), "wk": w[:, :, DH:2 * DH].reshape(D, HEADS * DH),
        "wv": w[:, :, 2 * DH:].reshape(D, HEADS * DH),
        "biases": np.stack([b[:, 0:DH].reshape(-1), b[:, DH:2 * DH].reshape(-1), a["L0_attn_bout"],
                            b[:, 2 * DH:].reshape(-1)]),
        "wout": a["L0_attn_Wout"].reshape(HEADS * DH, D),
        "w_gate": a["L0_ffn_w_gate"], "wi_0": a["L0_ffn_wi_0"], "wi_1": a["L0_ffn_wi_1"], "wo": a["L0_ffn_wo"],
    }
    nc = bacc.Bacc("TRN2", target_bir_lowering=False, num_devices=1)
    dram = {}
    for name in list(arrays):
        arrays["in_" + name] = np.ascontiguousarray(arrays.pop(name))
        dram[name] = nc.dram_tensor("in_" + name, arrays["in_" + name].shape, F32, kind="ExternalInput").ap()
    dram["out"] = nc.dram_tensor("out", [TOKENS, D], F32, kind="ExternalOutput").ap()
    build(nc, dram)
    r = run_bass_kernel_spmd(nc, [arrays], core_ids=[0])
    return np.asarray(r.results[0]["out"]).reshape(BATCH, SEQ, D)
```
